# Optimizing a Trainium2 kernel written in Bass

```python
import numpy as np
import jax
import jax.numpy as jnp

def _softmax(x, axis=-1):
    return jax.nn.softmax(x, axis=axis)

def _gelu(x):
    return jax.nn.gelu(x, approximate=True)

def _silu(x):
    return jax.nn.silu(x)

def _sigmoid(x):
    return jax.nn.sigmoid(x)

def _layernorm(x, axis=-1, eps=1e-05):
    m = jnp.mean(x, axis=axis, keepdims=True)
    v = jnp.var(x, axis=axis, keepdims=True)
    return (x - m) / jnp.sqrt(v + eps)

def _scatter_add(tgt, idx, src, axis=0):
    return tgt.at[idx].add(src)

def _segment_sum(src, seg, n):
    return jax.ops.segment_sum(src, seg, n)
kernel_name = 'mk_xattn_ffn_d1_seqx_r2_f3125f'

def setup_inputs(seed: int=0):
    np.random.seed(seed)
    _w = jnp.asarray

    def _rec_inputs():
        import jax
        import jax.numpy as jnp
        _rk = jax.random.key(seed)
        x = -0.0005207 + 1.001 * jax.random.normal(jax.random.fold_in(_rk, 1), (8, 512, 512), jnp.float32)
        _lenS = 512 - jax.random.randint(jax.random.fold_in(_rk, 7), (8,), 0, max(1, 512 // 4) + 1, jnp.int32)
        _lenS2 = 512 - jax.random.randint(jax.random.fold_in(_rk, 8), (8,), 0, max(1, 512 // 4) + 1, jnp.int32)
        _ctx_1024P = jax.random.normal(jax.random.fold_in(_rk, 11), (8, 16, 512), jnp.float32)
        _ctx_1024c = jax.random.dirichlet(jax.random.fold_in(_rk, 511), 0.3 * jnp.ones((16,), jnp.float32), (8, 512))
        _ctx_1024t = jnp.einsum('bsk,bkd->bsd', _ctx_1024c, _ctx_1024P)
        _ctx_1024t = _ctx_1024t * jax.lax.rsqrt(jnp.mean(jnp.square(_ctx_1024t)) + 1e-12) * 0.953939
        ctx_1024 = -0.000514642 + 1.00011 * (_ctx_1024t + 0.3 * jax.random.normal(jax.random.fold_in(_rk, 611), (8, 512, 512), jnp.float32))
        _validS = jnp.arange(512)[None, :] < _lenS[:, None]
        _validS2 = jnp.arange(512)[None, :] < _lenS2[:, None]
        _causal = jnp.tril(jnp.ones((512, 512), dtype=bool))
        mask_1x1xSxS2_ik0 = jnp.where(jnp.broadcast_to(_validS2[0:1, None, None, :], (1, 1, 512, 512)), 0, 1).astype(jnp.int32)
        return (x, ctx_1024, mask_1x1xSxS2_ik0)
    x, ctx_1024, mask_1x1xSxS2_ik0 = _rec_inputs()

    def _L0_xattn_setup():
        import jax, jax.numpy as jnp
        import numpy as np
        import math
        D = 512
        H = 16
        KVH = 2
        DK = D // H
        REP = H // KVH

        def _rope(x, pos):
            dk = x.shape[-1]
            inv_freq = 1.0 / 10000.0 ** (jnp.arange(0, dk, 2, dtype=jnp.float32) / dk)
            freqs = pos.astype(jnp.float32)[:, None] * inv_freq[None, :]
            cos = jnp.cos(freqs)
            sin = jnp.sin(freqs)
            x1, x2 = jnp.split(x, 2, axis=-1)
            return jnp.concatenate([x1 * cos - x2 * sin, x2 * cos + x1 * sin], axis=-1)
        key = jax.random.key(seed)
        ks = jax.random.split(key, 7)
        B, L = (1, 1024)
        q = jax.random.normal(ks[0], (B, L, D), jnp.float32)
        k = jax.random.normal(ks[1], (B, L, D), jnp.float32)
        v = jax.random.normal(ks[2], (B, L, D), jnp.float32)
        mask = jnp.tril(jnp.ones((L, L), jnp.int32))[None, None]
        s = 1.0 / math.sqrt(D)
        wq = jax.random.normal(ks[3], (D, D), jnp.float32) * s
        wk = jax.random.normal(ks[4], (D, D // REP), jnp.float32) * s
        wv = jax.random.normal(ks[5], (D, D // REP), jnp.float32) * s
        wo = jax.random.normal(ks[6], (D, D), jnp.float32) * s
        return {'query': q, 'key': k, 'value': v, 'mask': mask, 'wq': wq, 'wk': wk, 'wv': wv, 'wo': wo}
    _L0_xattn_all = _L0_xattn_setup()
    _L0_xattn_in = {k: v for k, v in _L0_xattn_all.items() if k in ('wq', 'wk', 'wv', 'wo')}
    del _L0_xattn_all

    def _L0_ffn_setup():
        import jax, jax.numpy as jnp
        import numpy as np
        B, S, D = (2, 512, 512)
        E, K, F, FS = (8, 2, 256, 512)
        key = jax.random.key(seed)
        ks = jax.random.split(key, 9)
        s = lambda k, shape, fan: jax.random.normal(k, shape, jnp.float32) * fan ** (-0.5)
        return {'x': jax.random.normal(ks[0], (B, S, D), jnp.float32), 'Wr': s(ks[1], (D, E), D), 'Wg': s(ks[2], (E, D, F), D), 'Wu': s(ks[3], (E, D, F), D), 'Wd': s(ks[4], (E, F, D), F), 'Sg': s(ks[5], (D, FS), D), 'Su': s(ks[6], (D, FS), D), 'Sd': s(ks[7], (FS, D), FS), 'expert_bias': jnp.zeros((E,), jnp.float32)}
    _L0_ffn_all = _L0_ffn_setup()
    _L0_ffn_in = {k: v for k, v in _L0_ffn_all.items() if k in ('Wr', 'Wg', 'Wu', 'Wd', 'Sg', 'Su', 'Sd', 'expert_bias')}
    del _L0_ffn_all
    return {'x': x, 'ctx_1024': ctx_1024, 'mask_1x1xSxS2_ik0': mask_1x1xSxS2_ik0, 'L0_xattn_wq': _L0_xattn_in['wq'], 'L0_xattn_wk': _L0_xattn_in['wk'], 'L0_xattn_wv': _L0_xattn_in['wv'], 'L0_xattn_wo': _L0_xattn_in['wo'], 'L0_ffn_Wr': _L0_ffn_in['Wr'], 'L0_ffn_Wg': _L0_ffn_in['Wg'], 'L0_ffn_Wu': _L0_ffn_in['Wu'], 'L0_ffn_Wd': _L0_ffn_in['Wd'], 'L0_ffn_Sg': _L0_ffn_in['Sg'], 'L0_ffn_Su': _L0_ffn_in['Su'], 'L0_ffn_Sd': _L0_ffn_in['Sd'], 'L0_ffn_expert_bias': _L0_ffn_in['expert_bias']}

def reference(x, ctx_1024, mask_1x1xSxS2_ik0, L0_xattn_wq, L0_xattn_wk, L0_xattn_wv, L0_xattn_wo, L0_ffn_Wr, L0_ffn_Wg, L0_ffn_Wu, L0_ffn_Wd, L0_ffn_Sg, L0_ffn_Su, L0_ffn_Sd, L0_ffn_expert_bias):
    import jax
    import jax.numpy as jnp

    def _L0_xattn_ref(query, key, value, mask, wq, wk, wv, wo):
        import jax, jax.numpy as jnp
        import numpy as np
        import math
        D = 512
        H = 16
        KVH = 2
        DK = D // H
        REP = H // KVH

        def _rope(x, pos):
            dk = x.shape[-1]
            inv_freq = 1.0 / 10000.0 ** (jnp.arange(0, dk, 2, dtype=jnp.float32) / dk)
            freqs = pos.astype(jnp.float32)[:, None] * inv_freq[None, :]
            cos = jnp.cos(freqs)
            sin = jnp.sin(freqs)
            x1, x2 = jnp.split(x, 2, axis=-1)
            return jnp.concatenate([x1 * cos - x2 * sin, x2 * cos + x1 * sin], axis=-1)
        B, L, _ = query.shape
        Q = (query @ wq).reshape(B, L, H, DK).transpose(0, 2, 1, 3)
        K = (key @ wk).reshape(B, L, KVH, DK).transpose(0, 2, 1, 3)
        V = (value @ wv).reshape(B, L, KVH, DK).transpose(0, 2, 1, 3)
        K = jnp.repeat(K, REP, axis=1)
        V = jnp.repeat(V, REP, axis=1)
        pos = jnp.arange(L)
        Q = _rope(Q, pos)
        K = _rope(K, pos)
        scores = jnp.einsum('bhqd,bhkd->bhqk', Q, K) / math.sqrt(DK)
        scores = jnp.where(mask == 0, -1000000000.0, scores)
        attn = jax.nn.softmax(scores, axis=-1)
        out = jnp.einsum('bhqk,bhkd->bhqd', attn, V)
        out = out.transpose(0, 2, 1, 3).reshape(B, L, H * DK)
        return out @ wo

    def _L0_ffn_ref(x, Wr, Wg, Wu, Wd, Sg, Su, Sd, expert_bias):
        import jax, jax.numpy as jnp
        import numpy as np
        B, S, D = (2, 512, 512)
        E, K, F, FS = (8, 2, 256, 512)
        b, s, d = x.shape
        xf = x.reshape(-1, d)
        T = xf.shape[0]
        logits = xf @ Wr + expert_bias
        top_v, top_i = jax.lax.top_k(logits, K)
        probs = jax.nn.softmax(top_v, axis=-1)
        rw = jnp.zeros_like(logits).at[jnp.arange(T)[:, None], top_i].set(probs)
        gate = jnp.einsum('td,edf->tef', xf, Wg)
        up = jnp.einsum('td,edf->tef', xf, Wu)
        h = jax.nn.silu(gate) * up
        eo = jnp.einsum('tef,efd->ted', h, Wd)
        out = jnp.einsum('te,ted->td', rw, eo)
        out = out + jax.nn.silu(xf @ Sg) * (xf @ Su) @ Sd
        return out.reshape(b, s, d)
    x = x + _L0_xattn_ref(_layernorm(x, axis=-1), ctx_1024, ctx_1024, mask_1x1xSxS2_ik0, L0_xattn_wq, L0_xattn_wk, L0_xattn_wv, L0_xattn_wo)
    x = x + _L0_ffn_ref(_layernorm(x, axis=-1), L0_ffn_Wr, L0_ffn_Wg, L0_ffn_Wu, L0_ffn_Wd, L0_ffn_Sg, L0_ffn_Su, L0_ffn_Sd, L0_ffn_expert_bias)
    return x

_drawn_inputs = setup_inputs


def setup_inputs(seed=0):
    import zlib

    import numpy as np

    out = dict(_drawn_inputs(seed))
    spreads = {'L0_ffn_expert_bias': (0.0, 0.1)}
    factors = {}
    for name, (base, spread) in spreads.items():
        noise = np.random.default_rng([zlib.crc32(name.encode()), seed]).standard_normal(out[name].shape)
        drawn = base * np.exp(spread * noise) if base else spread * noise
        out[name] = jnp.asarray(drawn.astype(out[name].dtype))
    for name, factor in factors.items():
        out[name] = (out[name] * factor).astype(out[name].dtype)
    return out
```

```python
import math
from contextlib import ExitStack

import numpy as np
import concourse.bass as bass
from concourse import mybir

F32, F32R, I32, U32 = mybir.dt.float32, mybir.dt.float32r, mybir.dt.int32, mybir.dt.uint32
ALU = mybir.AluOpType
ACT = mybir.ActivationFunctionType

P = 128
B, L, D = 8, 512, 512
TOKENS = B * L
TILES = TOKENS // P
TT = L // P
DC = D // P
H, KVH, DK = 16, 2, 32
REP = H // KVH
KV = KVH * DK
GH = P // DK
HG = H // GH
RING = GH + 1
E, F, FS = 8, 256, 512
FC = F // P
CW = 2 * F + D // FC
VISITS = TOKENS * 2 // P + E
SLOTS = E * TOKENS + (VISITS + 1) * P
NO_TOKEN = 1 << 20
EPS = 1e-5
MASKED = 2.0 ** 100
HUGE = 3.0e38


def twice(tile, heads):
    return tile[:].rearrange("p (h d) -> p h d", h=heads).unsqueeze(2).broadcast_to([P, heads, 2, DK])


def alone(eng, passed):
    eng.sem_inc(passed, 1)


def tables(nc):
    pos = np.arange(L, dtype=np.float32)
    inv_freq = (1.0 / 10000.0 ** (np.arange(0, DK, 2, dtype=np.float32) / DK)).astype(np.float32)
    freqs = pos[:, None] * inv_freq[None, :]
    cos, sin = np.cos(freqs), np.sin(freqs)
    rope = np.stack([np.concatenate([cos, cos], 1), np.concatenate([-sin, sin], 1)], 1).astype(np.float32)
    rope = np.ascontiguousarray(rope.reshape(TT, P, 2, DK).transpose(1, 0, 2, 3))
    pick = np.zeros((2 * GH, P), np.float32)
    for r in range(2 * GH):
        pick[r, DK * (r % GH):DK * (r % GH + 1)] = 1.0
    def constant(name, array):
        return nc.inline_tensor(array.astype(np.float32), name=name).ap()

    return dict(
        ident=constant("c_ident", np.eye(P)),
        pick=constant("c_pick", pick),
        ones=constant("c_ones", np.ones((P, P))),
        tri=constant("c_tri", np.triu(np.ones((P, P)), 1)),
        columns=constant("c_columns", np.concatenate([np.arange(P)[:, None], np.tile(np.arange(E), (P, 1))], 1)),
        rope_k=constant("c_rope_k", rope),
        rope_q=constant("c_rope_q", -rope / math.sqrt(DK)),
    )


def attention_phase(nc, k, x_rows, ctx_rows, mask, wq, wk, wv, wo, x2_rows):
    with ExitStack() as ctx:
        def sb(name, shape, dt=F32):
            return ctx.enter_context(nc.sbuf_tensor("a_" + name, shape, dt))

        def sem(name):
            return ctx.enter_context(nc.semaphore("a_" + name))

        ident = sb("ident", [P, P])
        ident_r = sb("ident_r", [P, P], F32R)
        pick_raw = sb("pick_raw", [2 * GH, P])
        pick = sb("pick", [2 * GH, P], F32R)
        half = sb("half", [P, 2])
        rope_q = sb("rope_q", [P, TT, 2, DK])
        rope_k = sb("rope_k", [P, TT, 2, DK])
        bias = sb("bias", [P, TT, L])
        wq_hi, wq_lo = sb("wq_hi", [P, DC, D], F32R), sb("wq_lo", [P, DC, D], F32R)
        wo_hi, wo_lo = sb("wo_hi", [P, DC, D], F32R), sb("wo_lo", [P, DC, D], F32R)
        wkv = sb("wkv", [P, DC, 2 * KV])
        x_in, ctx_in, x_res = sb("x_in", [P, 2, D]), sb("ctx_in", [P, 2, D]), sb("x_res", [P, 2, D])
        x2 = sb("x2", [P, 2, D])
        stats, moments, rstd = sb("stats", [P, 6]), sb("moments", [P, 2]), sb("rstd", [P, 2])
        xn = sb("xn", [P, D])
        xnT_hi, xnT_lo = sb("xnT_hi", [P, 2, D], F32R), sb("xnT_lo", [P, 2, D], F32R)
        ctxT = sb("ctxT", [P, 2, D])
        rot_a, rot_b = sb("rot_a", [P, D]), sb("rot_b", [P, D])
        q_stack = sb("q_stack", [P, H, 4, DK], F32R)
        k_stack = sb("k_stack", [P, KVH, 4, DK], F32R)
        qT = sb("qT", [P, H, L], F32R)
        kT = sb("kT", [P, KVH, L], F32R)
        v = sb("v", [P, TT, KV])
        low = sb("low", [P, H, TT])
        total = sb("total", [P, 2, TT, GH])
        inverse = sb("inverse", [P, TT, GH])
        inverse_hl = sb("inverse_hl", [P, TT, 2, GH], F32R)
        inverseT = sb("inverseT", [2 * GH, L], F32R)
        spread = sb("spread", [P, L])
        probs = sb("probs", [P, 2, TT, L])
        probsT = sb("probsT", [P, RING, TT, L])
        att = sb("att", [P, L])
        attT_hi, attT_lo = sb("attT_hi", [P, HG, L], F32R), sb("attT_lo", [P, HG, L], F32R)
        psum = ctx.enter_context(nc.psum_tensor("a_psum", [P, 8, 512], F32))

        const_in, kv_in, wq_in, wo_in, mask_in = (sem(n) for n in "const_in kv_in wq_in wo_in mask_in".split())
        wq_rounded, wq_split, wo_rounded, wo_split = (sem(n) for n in "wq_rounded wq_split wo_rounded wo_split".split())
        consts_ready, half_ready, bias_ready = sem("consts_ready"), sem("half_ready"), sem("bias_ready")
        x_loaded, ctx_loaded, res_loaded = ([sem(f"{n}{i}") for i in range(2)] for n in ("x_in", "ctx_in", "x_res"))
        stored = [sem(f"stored{i}") for i in range(2)]
        x_used, ctx_used, res_used = sem("x_used"), sem("ctx_used"), sem("res_used")
        xT_rounded = sem("xT_rounded")
        moments_ready, rstd_ready, xn_ready = sem("moments_ready"), sem("rstd_ready"), sem("xn_ready")
        filled, freed_act, freed_vec = sem("filled"), sem("freed_act"), sem("freed_vec")
        q_rotated, q_rounded, q_ready = sem("q_rotated"), sem("q_rounded"), sem("q_ready")
        k_ready = sem("k_ready")
        s_filled, s_freed, low_ready, probs_ready = sem("s_filled"), sem("s_freed"), sem("low_ready"), sem("probs_ready")
        t_filled, t_freed_act, t_freed_vec = sem("t_filled"), sem("t_freed_act"), sem("t_freed_vec")
        inverse_ready, spread_ready, out_filled, att_ready = (sem(n) for n in "inverse_ready spread_ready out_filled att_ready".split())
        att_rounded, att_split = sem("att_rounded"), sem("att_split")
        vec_step, passed = sem("vec_step"), sem("passed")

        OUT_BANK = 5

        def t_bank(h, c):
            return 2 + (TT * h + c) % 3

        def evacuated_by_act(h, c):
            return c in (0, 2) or (c == 1 and h % 2 == 0)

        def evacuated(h, c, act):
            return sum(evacuated_by_act(i // TT, i % TT) == act for i in range(TT * h + c + 1))

        turns = []
        for s in range(TT + 2):
            if s < TT:
                turns += [(("xT", s), "vec"), (("ctxT", s), "act")]
            if s >= 2:
                turns += [(("qT", s - 2, i), "act") for i in range(HG)] + [(("kT", s - 2), "vec")]
            if 1 <= s <= TT:
                turns += [(("q", s - 1), "vec"), (("kv", s - 1), "vec")]
        for g in range(HG):
            turns += [(("inverse", g), "act"), (("spread", g), "act")]
        turns += [(("wo", t), "vec") for t in range(TT)]
        TURNS = len(turns)
        assert TURNS % 2 == 0
        turn = {name: i for i, (name, _) in enumerate(turns)}
        by = [engine for _, engine in turns]
        ACT_TURNS, VEC_TURNS = by.count("act"), by.count("vec")

        def bank(name):
            return psum[:, 6 + turn[name] % 2, :]

        def wait_filled(eng, b, name):
            eng.wait_ge(filled, b * TURNS + turn[name] + 1)

        def wait_free(eng, b, name):
            i = turn[name] - 2
            if i >= 0:
                n = by[:i + 1].count(by[i])
                if by[i] == "act":
                    eng.wait_ge(freed_act, b * ACT_TURNS + n)
                else:
                    eng.wait_ge(freed_vec, b * VEC_TURNS + n)

        ET = evacuated(H - 1, TT - 1, True)
        VT = evacuated(H - 1, TT - 1, False)

        with nc.Block() as block:
            @block.sync
            def _(sp):
                for i in range(2):
                    sp.sem_inc(stored[i], 16)
                for dst, src in ((ident, k["ident"]), (pick_raw, k["pick"]), (rope_q, k["rope_q"]), (rope_k, k["rope_k"])):
                    sp.dma_start(dst[:], src).then_inc(const_in, 16)
                wq_raw, wo_raw = probs[:, 0], probs[:, 1]
                sp.dma_start(wq_raw, wq.rearrange("(c p) n -> p c n", p=P)).then_inc(wq_in, 16)
                sp.dma_start(wo_raw, wo.rearrange("(c p) n -> p c n", p=P)).then_inc(wo_in, 16)
                sp.dma_start(wkv[:, :, 0:KV], wk.rearrange("(c p) n -> p c n", p=P)).then_inc(kv_in, 16)
                sp.dma_start(wkv[:, :, KV:2 * KV], wv.rearrange("(c p) n -> p c n", p=P)).then_inc(kv_in, 16)
                sp.dma_start(probsT[:, 0].bitcast(I32), mask.rearrange("a b (t p) k -> p (a b t) k", p=P)).then_inc(mask_in, 16)
                with sp.Fori(0, B) as b:
                    for t in range(TT):
                        sp.wait_ge(x_used, b * TT + t + 1)
                        sp.dma_start(x_in[:, t % 2], x_rows[b * TT + t]).then_inc(x_loaded[t % 2], 16)
                        sp.wait_ge(ctx_used, b * TT + t + 1)
                        sp.dma_start(ctx_in[:, t % 2], ctx_rows[b * TT + t]).then_inc(ctx_loaded[t % 2], 16)
                    for t in range(2):
                        sp.wait_ge(res_used, b * TT + t + 1)
                        sp.dma_start(x_res[:, t], x_rows[b * TT + t]).then_inc(res_loaded[t], 16)
                    for t in range(TT):
                        sp.wait_ge(res_used, b * TT + t + 3)
                        if t + 2 < TT:
                            sp.dma_start(x_res[:, t % 2], x_rows[b * TT + t + 2]).then_inc(res_loaded[t % 2], 16)
                        sp.dma_start(x2_rows[b * TT + t], x2[:, t % 2]).then_inc(stored[t % 2], 16)
                for i in range(2):
                    sp.wait_ge(stored[i], 16 + 16 * B * TT // 2)

            @block.gpsimd
            def _(pool):
                pool.memset(half[:], -0.5).then_inc(half_ready, 1)
                pool.wait_ge(half_ready, 1)
                with pool.Fori(0, B) as b:
                    for t in range(TT):
                        pool.wait_ge(moments_ready, b * TT + t + 1)
                        nc.gpsimd.tensor_tensor(rstd[:, t % 2:t % 2 + 1], moments[:, 1:2], half[:, 0:1], ALU.pow).then_inc(rstd_ready, 1)

            @block.scalar
            def _(act):
                act.sem_inc(ctx_used, 2)
                act.wait_ge(wq_in, 16)
                nc.scalar.activation(wq_hi[:], probs[:, 0], ACT.Copy).then_inc(wq_rounded, 1)
                act.wait_ge(wo_in, 16)
                nc.scalar.activation(wo_hi[:], probs[:, 1], ACT.Copy).then_inc(wo_rounded, 1)
                with act.Fori(0, B) as b:
                    def copy(dst, name, then):
                        wait_filled(act, b, name)
                        nc.scalar.activation(dst, bank(name), ACT.Copy).then_inc(then, 1)

                    for s in range(TT + 2):
                        if s < TT:
                            wait_filled(act, b, ("xT", s))
                            nc.scalar.activation(xnT_hi[:, s % 2], bank(("xT", s)), ACT.Copy).then_inc(xT_rounded, 1)
                            wait_filled(act, b, ("ctxT", s))
                            act.sem_inc(ctx_used, 1)
                            nc.scalar.activation(ctxT[:, s % 2], bank(("ctxT", s)), ACT.Copy).then_inc(freed_act, 1)
                        if s >= 2:
                            for i in range(HG):
                                wait_filled(act, b, ("qT", s - 2, i))
                                nc.scalar.activation(qT[:, GH * i:GH * (i + 1), P * (s - 2):P * (s - 1)],
                                                     bank(("qT", s - 2, i)).rearrange("p (h t) -> p h t", h=GH), ACT.Copy).then_inc(freed_act, 1)
                        if 1 <= s <= TT:
                            act.wait_ge(q_rotated, b * TT + s)
                            nc.scalar.activation(q_stack[:, :, 0:2], twice(rot_a, H), ACT.Copy).then_inc(q_rounded, 1)

                    def exps(h):
                        for t in range(TT):
                            act.wait_ge(low_ready, b * H * TT + TT * h + t + 1)
                            if h % GH == 0 and t == 0 and h >= 2 * GH:
                                act.wait_ge(inverse_ready, b * HG + h // GH - 1)
                            nc.scalar.activation(probs[:, h % 2, t], probs[:, h % 2, t], ACT.Exp, bias=low[:, h, t:t + 1], scale=-1.0,
                                                 accum_out=total[:, h // GH % 2, t, h % GH:h % GH + 1]).then_inc(probs_ready, 1)

                    exps(0)
                    for h in range(H):
                        if h + 1 < H:
                            exps(h + 1)
                        for c in range(TT):
                            if evacuated_by_act(h, c):
                                act.wait_ge(t_filled, b * H * TT + TT * h + c + 1)
                                nc.scalar.activation(probsT[:, h % RING, c], psum[:, t_bank(h, c)], ACT.Copy).then_inc(t_freed_act, 1)
                        if h % GH == GH - 1:
                            g = h // GH
                            wait_filled(act, b, ("inverse", g))
                            nc.scalar.activation(inverseT[:], bank(("inverse", g))[0:2 * GH], ACT.Copy).then_inc(freed_act, 1)
                            wait_filled(act, b, ("spread", g))
                            if g >= 1:
                                act.wait_ge(att_ready, b * HG + g)
                            nc.scalar.activation(spread[:], bank(("spread", g)), ACT.Copy).then_inc(freed_act, 1)
                        if h % GH == 0 and h > 0:
                            act.wait_ge(att_ready, b * HG + h // GH)
                            nc.scalar.activation(attT_hi[:, h // GH - 1], att[:], ACT.Copy).then_inc(att_rounded, 1)
                    act.wait_ge(att_ready, b * HG + HG)
                    nc.scalar.activation(attT_hi[:, HG - 1], att[:], ACT.Copy).then_inc(att_rounded, 1)

            @block.tensor
            def _(pe):
                pe.wait_ge(consts_ready, 2)
                pe.wait_ge(kv_in, 32)
                pe.wait_ge(wq_split, 1)
                pe.wait_ge(wo_split, 1)
                with pe.Fori(0, B) as b:
                    def turn4(name, src, identity, typed=lambda ap: ap):
                        wait_free(pe, b, name)
                        out = typed(bank(name))
                        for i in range(4):
                            last = nc.tensor.transpose(out[:, P * i:P * (i + 1)], src(i), identity[:])
                        last.then_inc(filled, 1)

                    def product(name, left_hi, left_lo, right_hi, right_lo):
                        wait_free(pe, b, name)
                        for c in range(DC):
                            nc.tensor.matmul(bank(name), left_hi(c), right_hi[:, c], start=(c == 0), stop=False)
                            nc.tensor.matmul(bank(name), left_hi(c), right_lo[:, c], start=False, stop=False)
                            last = nc.tensor.matmul(bank(name), left_lo(c), right_hi[:, c], start=False, stop=(c == DC - 1))
                        last.then_inc(filled, 1)

                    for s in range(TT + 2):
                        if s < TT:
                            pe.wait_ge(xn_ready, b * TT + s + 1)
                            turn4(("xT", s), lambda i: xn[:, P * i:P * (i + 1)], ident)
                            pe.wait_ge(ctx_loaded[s % 2], b * 32 + 16 * (s // 2) + 16)
                            turn4(("ctxT", s), lambda i: ctx_in[:, s % 2, P * i:P * (i + 1)], ident)
                        if s >= 2:
                            t = s - 2
                            pe.wait_ge(q_ready, b * TT + t + 1)
                            for g in range(HG):
                                turn4(("qT", t, g), lambda i: q_stack[:, GH * g + i].rearrange("p r d -> p (r d)"), ident_r,
                                      lambda ap: ap.bitcast(F32R))
                            pe.wait_ge(k_ready, b * TT + t + 1)
                            wait_free(pe, b, ("kT", t))
                            for i in range(KVH):
                                last = nc.tensor.transpose(bank(("kT", t))[:, P * i:P * (i + 1)].bitcast(F32R),
                                                           k_stack[:, i].rearrange("p r d -> p (r d)"), ident_r[:])
                            last.then_inc(filled, 1)
                        if 1 <= s <= TT:
                            t = s - 1
                            pe.wait_ge(xT_rounded, b * TT + t + 1)
                            pe.wait_ge(freed_vec, b * VEC_TURNS + by[:turn[("xT", t)] + 1].count("vec"))
                            product(("q", t), lambda c: xnT_hi[:, t % 2, P * c:P * (c + 1)], lambda c: xnT_lo[:, t % 2, P * c:P * (c + 1)], wq_hi, wq_lo)
                            wait_free(pe, b, ("kv", t))
                            pe.wait_ge(freed_act, b * ACT_TURNS + by[:turn[("ctxT", t)] + 1].count("act"))
                            for c in range(DC):
                                last = nc.tensor.matmul(bank(("kv", t))[:, 0:2 * KV], ctxT[:, t % 2, P * c:P * (c + 1)], wkv[:, c], start=(c == 0), stop=(c == DC - 1))
                            last.then_inc(filled, 1)

                    def scores(h):
                        if h == 0:
                            pe.wait_ge(freed_act, b * ACT_TURNS + by[:turn[("qT", TT - 1, HG - 1)] + 1].count("act"))
                            pe.wait_ge(freed_vec, b * VEC_TURNS + by[:turn[("kT", TT - 1)] + 1].count("vec"))
                        for t in range(TT):
                            if TT * h + t >= 2:
                                pe.wait_ge(low_ready, b * H * TT + TT * h + t - 1)
                            nc.tensor.matmul(psum[:, t % 2], qT[:, h, P * t:P * (t + 1)], kT[:, h // REP], start=True, stop=True).then_inc(s_filled, 1)

                    def transposes(h):
                        for c in range(TT):
                            if TT * h + c >= 3:
                                o = TT * h + c - 3
                                act_did = evacuated_by_act(o // TT, o % TT)
                                n = evacuated(o // TT, o % TT, act_did)
                                if act_did:
                                    pe.wait_ge(t_freed_act, b * ET + n)
                                else:
                                    pe.wait_ge(t_freed_vec, b * VT + n)
                            for t in range(TT):
                                if c == 0:
                                    pe.wait_ge(probs_ready, b * H * TT + TT * h + t + 1)
                                last = nc.tensor.transpose(psum[:, t_bank(h, c), P * t:P * (t + 1)], probs[:, h % 2, t, P * c:P * (c + 1)], ident[:])
                            last.then_inc(t_filled, 1)

                    def weighted(g):
                        last_h = GH * g + GH - 1
                        pe.wait_ge(t_freed_act, b * ET + evacuated(last_h, TT - 1, True))
                        pe.wait_ge(t_freed_vec, b * VT + evacuated(last_h, TT - 1, False))
                        if g >= 1:
                            pe.wait_ge(att_ready, b * HG + g)
                        for c in range(TT):
                            for j in range(GH):
                                h = GH * g + j
                                last = nc.tensor.matmul(psum[DK * j:DK * (j + 1), OUT_BANK], v[:, c, DK * (h // REP):DK * (h // REP + 1)],
                                                        probsT[:, h % RING, c], start=(c == 0), stop=(c == TT - 1))
                        last.then_inc(out_filled, 1)

                    scores(0)
                    for h in range(H):
                        if h + 1 < H:
                            scores(h + 1)
                        transposes(h)
                        if h % GH == GH - 1:
                            g = h // GH
                            pe.wait_ge(inverse_ready, b * HG + g + 1)
                            wait_free(pe, b, ("inverse", g))
                            for t in range(TT):
                                last = nc.tensor.transpose(bank(("inverse", g))[0:2 * GH, P * t:P * (t + 1)].bitcast(F32R),
                                                           inverse_hl[:, t].rearrange("p r h -> p (r h)"), ident_r[:])
                            last.then_inc(filled, 1)
                            pe.wait_ge(freed_act, b * ACT_TURNS + by[:turn[("inverse", g)] + 1].count("act"))
                            wait_free(pe, b, ("spread", g))
                            nc.tensor.matmul(bank(("spread", g)), pick[:], inverseT[:], start=True, stop=True).then_inc(filled, 1)
                        if h % GH == 0 and h > 0:
                            weighted(h // GH - 1)
                    weighted(HG - 1)
                    pe.wait_ge(att_rounded, b * HG + HG)
                    pe.wait_ge(att_split, b * HG + HG)
                    for t in range(TT):
                        product(("wo", t), lambda c: attT_hi[:, c, P * t:P * (t + 1)], lambda c: attT_lo[:, c, P * t:P * (t + 1)], wo_hi, wo_lo)

            @block.vector
            def _(dve):
                steps = [0]
                base = [0]

                def step(ins):
                    steps[0] += 1
                    ins.then_inc(vec_step, 1)
                    dve.wait_ge(vec_step, base[0] + steps[0])

                dve.sem_inc(x_used, 2)
                dve.sem_inc(res_used, 2)
                dve.wait_ge(const_in, 64)
                nc.vector.tensor_copy(ident_r[:], ident[:]).then_inc(consts_ready, 1)
                nc.vector.tensor_copy(pick[:], pick_raw[:]).then_inc(consts_ready, 1)
                dve.wait_ge(wq_rounded, 1)
                nc.vector.tensor_tensor(wq_lo[:], probs[:, 0], wq_hi[:].bitcast(F32), ALU.subtract).then_inc(wq_split, 1)
                dve.wait_ge(wo_rounded, 1)
                nc.vector.tensor_tensor(wo_lo[:], probs[:, 1], wo_hi[:].bitcast(F32), ALU.subtract).then_inc(wo_split, 1)
                dve.wait_ge(mask_in, 16)
                step(nc.vector.tensor_scalar(bias[:], probsT[:, 0].bitcast(I32), 0.0, MASKED, ALU.is_equal, ALU.mult))
                base[0] = steps[0]
                steps[0] = 0
                with dve.Fori(0, B) as b:
                    base[0] = b * VEC_STEPS + base[0]

                    def normalise(t):
                        dve.wait_ge(x_loaded[t % 2], b * 32 + 16 * (t // 2) + 16)
                        step(nc.vector.bn_stats(stats[:], x_in[:, t % 2]))
                        alone(dve, passed)
                        step(nc.vector.bn_aggr(moments[:], stats[:]))
                        nc.vector.tensor_scalar(moments[:, 1:2], moments[:, 1:2], EPS, None, ALU.add).then_inc(moments_ready, 1)
                        dve.wait_ge(rstd_ready, b * TT + t + 1)
                        nc.vector.tensor_scalar(xn[:], x_in[:, t % 2], moments[:, 0:1], rstd[:, t % 2:t % 2 + 1], ALU.subtract, ALU.mult).then_inc(xn_ready, 1)
                        dve.wait_ge(xn_ready, b * TT + t + 1)
                        dve.sem_inc(x_used, 1)

                    def rotate(src, table, t, heads, a, c):
                        s = src.rearrange("p (h r d) -> p h r d", h=heads, r=2)
                        cos = table[:, t, 0].unsqueeze(1).broadcast_to([P, heads, DK])
                        sin = table[:, t, 1].rearrange("p (r d) -> p r d", r=2)
                        n = heads * DK
                        nc.vector.tensor_tensor(a[:, 0:n].rearrange("p (h d) -> p h d", h=heads), src.rearrange("p (h d) -> p h d", h=heads), cos, ALU.mult)
                        o = c[:, 0:n].rearrange("p (h r d) -> p h r d", h=heads, r=2)
                        nc.vector.tensor_tensor(o[:, :, 0], s[:, :, 1], sin[:, 0].unsqueeze(1).broadcast_to([P, heads, DK // 2]), ALU.mult)
                        return nc.vector.tensor_tensor(o[:, :, 1], s[:, :, 0], sin[:, 1].unsqueeze(1).broadcast_to([P, heads, DK // 2]), ALU.mult)

                    normalise(0)
                    for s in range(TT + 2):
                        if s < TT:
                            name = ("xT", s)
                            wait_filled(dve, b, name)
                            dve.wait_ge(xT_rounded, b * TT + s + 1)
                            nc.vector.tensor_tensor(xnT_lo[:, s % 2], bank(name), xnT_hi[:, s % 2].bitcast(F32), ALU.subtract).then_inc(freed_vec, 1)
                        if s + 1 < TT:
                            normalise(s + 1)
                        if s >= 2:
                            name = ("kT", s - 2)
                            wait_filled(dve, b, name)
                            nc.vector.tensor_copy(kT[:, :, P * (s - 2):P * (s - 1)], bank(name)[:, 0:KVH * P].rearrange("p (h t) -> p h t", h=KVH)).then_inc(freed_vec, 1)
                        if 1 <= s <= TT:
                            t = s - 1
                            name = ("q", t)
                            wait_filled(dve, b, name)
                            rotate(bank(name), rope_q, t, H, rot_a, rot_b).then_inc(freed_vec, 1)
                            dve.wait_ge(freed_vec, b * VEC_TURNS + by[:turn[name] + 1].count("vec"))
                            nc.vector.tensor_tensor(rot_a[:], rot_a[:], rot_b[:], ALU.add).then_inc(q_rotated, 1)
                            dve.wait_ge(q_rounded, b * TT + t + 1)
                            nc.vector.tensor_tensor(q_stack[:, :, 2:4], twice(rot_a, H), q_stack[:, :, 0:2].bitcast(F32), ALU.subtract).then_inc(q_ready, 1)
                            dve.wait_ge(q_ready, b * TT + t + 1)
                            name = ("kv", t)
                            wait_filled(dve, b, name)
                            step(rotate(bank(name)[:, 0:KV], rope_k, t, KVH, rot_a, rot_b))
                            nc.vector.tensor_copy(v[:, t], bank(name)[:, KV:2 * KV]).then_inc(freed_vec, 1)
                            step(nc.vector.tensor_tensor(rot_a[:, 0:KV], rot_a[:, 0:KV], rot_b[:, 0:KV], ALU.add))
                            kr = rot_a[:, 0:KV].rearrange("p (h d) -> p h d", h=KVH)
                            step(nc.vector.tensor_copy(k_stack[:, :, 0], kr))
                            step(nc.vector.tensor_tensor(k_stack[:, :, 1], kr, k_stack[:, :, 0].bitcast(F32), ALU.subtract))
                            nc.vector.tensor_copy(k_stack[:, :, 2:4], k_stack[:, :, 0:2].bitcast(F32)).then_inc(k_ready, 1)

                    def lows(h):
                        for t in range(TT):
                            dve.wait_ge(s_filled, b * H * TT + TT * h + t + 1)
                            if h >= 2 and t == 0:
                                dve.wait_ge(t_filled, b * H * TT + TT * (h - 1))
                            alone(dve, passed)
                            nc.vector.tensor_tensor_reduce(probs[:, h % 2, t], psum[:, t % 2], bias[:, t], 1.0, HUGE, ALU.add, ALU.min,
                                                           low[:, h, t:t + 1]).then_inc(low_ready, 1)

                    def scale_group(g):
                        wait_filled(dve, b, ("spread", g))
                        dve.wait_ge(out_filled, b * HG + g + 1)
                        dve.wait_ge(freed_act, b * ACT_TURNS + by[:turn[("spread", g)] + 1].count("act"))
                        if g >= 1:
                            dve.wait_ge(att_rounded, b * HG + g)
                        nc.vector.tensor_tensor(att[:], psum[:, OUT_BANK], spread[:], ALU.mult).then_inc(att_ready, 1)
                        dve.wait_ge(att_rounded, b * HG + g + 1)
                        nc.vector.tensor_tensor(attT_lo[:, g], att[:], attT_hi[:, g].bitcast(F32), ALU.subtract).then_inc(att_split, 1)
                        dve.wait_ge(att_split, b * HG + g + 1)

                    lows(0)
                    for h in range(H):
                        if h + 1 < H:
                            lows(h + 1)
                        for c in range(TT):
                            if not evacuated_by_act(h, c):
                                dve.wait_ge(t_filled, b * H * TT + TT * h + c + 1)
                                nc.vector.tensor_copy(probsT[:, h % RING, c], psum[:, t_bank(h, c)]).then_inc(t_freed_vec, 1)
                        if h % GH == GH - 1:
                            g = h // GH
                            dve.wait_ge(probs_ready, b * H * TT + TT * (h + 1))
                            step(nc.vector.reciprocal(inverse[:], total[:, g % 2]))
                            step(nc.vector.tensor_copy(inverse_hl[:, :, 0], inverse[:]))
                            nc.vector.tensor_tensor(inverse_hl[:, :, 1], inverse[:], inverse_hl[:, :, 0].bitcast(F32), ALU.subtract).then_inc(inverse_ready, 1)
                        if h % GH == 0 and h > 0:
                            scale_group(h // GH - 1)
                    scale_group(HG - 1)
                    for t in range(TT):
                        name = ("wo", t)
                        wait_filled(dve, b, name)
                        dve.wait_ge(res_loaded[t % 2], b * 32 + 16 * (t // 2) + 16)
                        dve.wait_ge(stored[t % 2], b * 32 + 16 * (t // 2) + 16)
                        nc.vector.tensor_tensor(x2[:, t % 2], bank(name), x_res[:, t % 2], ALU.add).then_inc(freed_vec, 1)
                        dve.wait_ge(freed_vec, b * VEC_TURNS + by[:turn[name] + 1].count("vec"))
                        dve.sem_inc(res_used, 1)
                    assert steps[0] == VEC_STEPS, steps[0]


def shared_phase(nc, k, x2_rows, xn_rows, out_rows, wr, sg, su, sd, expert_bias, wg, wu, wd, pairs, halves, tile_table):
    with ExitStack() as ctx:
        def sb(name, shape, dt=F32):
            return ctx.enter_context(nc.sbuf_tensor("b_" + name, shape, dt))

        def sem(name):
            return ctx.enter_context(nc.semaphore("b_" + name))

        ident, tri, ones = sb("ident", [P, P]), sb("tri", [P, P]), sb("ones", [P, P])
        columns = sb("columns", [P, 1 + E])
        half = sb("half", [P, 1])
        raw = sb("raw", [P, 2, DC, D])
        sg_hi, sg_lo = sb("sg_hi", [P, DC, D], F32R), sb("sg_lo", [P, DC, D], F32R)
        su_hi, su_lo = sb("su_hi", [P, DC, D], F32R), sb("su_lo", [P, DC, D], F32R)
        sd_hi, sd_lo = sb("sd_hi", [P, DC, D], F32R), sb("sd_lo", [P, DC, D], F32R)
        wr_raw, wr_hi, wr_lo = sb("wr_raw", [P, DC, E]), sb("wr_hi", [P, DC, E], F32R), sb("wr_lo", [P, DC, E], F32R)
        router_bias = sb("router_bias", [P, E])
        unused = sb("unused", [P, SLOTS // P, 2], I32)
        x_in, x_res, acc = sb("x_in", [P, 2, D]), sb("x_res", [P, 2, D]), sb("acc", [P, 2, D])
        stats, moments, rstd = sb("stats", [P, 6]), sb("moments", [P, 2]), sb("rstd", [P, 2])
        xn = sb("xn", [P, 2, D])
        xT_hi, xT_lo = sb("xT_hi", [P, D], F32R), sb("xT_lo", [P, D], F32R)
        act_half, hidden = sb("act_half", [P, FS]), sb("hidden", [P, FS])
        hT_hi, hT_lo = sb("hT_hi", [P, FS], F32R), sb("hT_lo", [P, FS], F32R)
        w_raw, w_hi, w_lo = sb("w_raw", [P, 2, CW]), sb("w_hi", [P, 2, CW], F32R), sb("w_lo", [P, 2, CW], F32R)
        logits, best, best_at, best_f = sb("logits", [P, E]), sb("best", [P, E]), sb("best_at", [P, E], U32), sb("best_f", [P, 2])
        chosen, picked, counted = sb("chosen", [P, 2, E]), sb("picked", [P, E]), sb("counted", [P, E])
        junk = sb("junk", [P, 2, E])
        gap, e_gap, gate_sum, gates, place = sb("gap", [P, 1]), sb("e_gap", [P, 1]), sb("gate_sum", [P, 1]), sb("gates", [P, 2]), sb("place", [P, 2])
        token = sb("token", [P, 1])
        slot_f, slot, pair = sb("slot_f", [P, 2]), sb("slot", [P, 2, 2], I32), sb("pair", [P, 2, 2, 2], I32)
        counts_i, n_tiles, ends, table_f, table = sb("counts_i", [P, 2, E], I32), sb("n_tiles", [P, E]), sb("ends", [P, 2, E]), sb("table_f", [P, 4]), sb("table", [P, 2], I32)
        before = sb("before", [P, 2, E])
        psum = ctx.enter_context(nc.psum_tensor("b_psum", [P, 8, 512], F32))
        XT, GATE, UP, DOWN, HT, LOGITS, RANK = 0, 1, 2, 3, 5, 6, 7

        names = "const_in consts_ready half_ready raw_in0 raw_in1 raw_in2 wr_in rounded split slots_clear clear_ready bias_in "
        names += "x_used res_used moments_ready rstd_ready xn_ready xT_filled xT_rounded xT_split gate_filled up_filled "
        names += "squashed gated hidden_ready hT_filled hT_rounded hT_split down_filled acc_ready logits_filled "
        names += "logits_ready picked_ready rank_filled gap_ready e_gap_ready pair_ready w_used w_ready w_stored table_ready table_out counts_filled "
        names += "vec_step pool_step passed pair_used"
        s = {n: sem(n) for n in names.split()}
        x_loaded, res_loaded, xn_stored, acc_stored, w_loaded, scattered = (
            [sem(f"{n}{i}") for i in range(2)] for n in ("x_in", "x_res", "xn_stored", "acc_stored", "w_in", "scattered"))

        def pipeline(eng, step):
            step(0, 0, True, False)
            with eng.Fori(0, (TILES - 2) // 2) as i:
                step(2 * i + 1, 1, False, False)
                step(2 * i + 2, 0, False, False)
            step(TILES - 1, 1, False, True)

        with nc.Block() as block:
            @block.sync
            def _(sp):
                for dst, src in ((ident, k["ident"]), (tri, k["tri"]), (ones, k["ones"]), (columns, k["columns"])):
                    sp.dma_start(dst[:], src).then_inc(s["const_in"], 16)
                for i in range(2):
                    sp.sem_inc(xn_stored[i], 16)
                    sp.sem_inc(acc_stored[i], 16)

                def load_x(n, q):
                    sp.wait_ge(s["x_used"], n + 1)
                    sp.dma_start(x_in[:, q], x2_rows[n % TILES]).then_inc(x_loaded[q], 16)

                load_x(0, 0)
                load_x(1, 1)
                sp.dma_start(raw[:, 0], sg.rearrange("(c p) n -> p c n", p=P)).then_inc(s["raw_in0"], 16)
                sp.dma_start(raw[:, 1], su.rearrange("(c p) n -> p c n", p=P)).then_inc(s["raw_in1"], 16)
                sp.dma_start(wr_raw[:], wr.rearrange("(c p) n -> p c n", p=P)).then_inc(s["wr_in"], 16)
                sp.dma_start(router_bias[:], expert_bias.rearrange("(a e) -> a e", a=1).broadcast_to([P, E])).then_inc(s["bias_in"], 16)
                sp.wait_ge(s["clear_ready"], 2)
                sp.dma_start(pairs.rearrange("(p s) w -> p s w", p=P), unused[:]).then_inc(s["slots_clear"], 16)
                sp.wait_ge(s["split"], 1)
                sp.dma_start(raw[:, 0], sd.rearrange("(c p) n -> p c n", p=P)).then_inc(s["raw_in2"], 16)

                wd_quarters = wd.rearrange("e f d -> e (f d)").rearrange("e (p c d) -> e c p d", p=P, c=DC)

                def load_w(n, q):
                    sp.wait_ge(s["w_used"], n + 1)
                    sp.dma_start(w_raw[:, q, 0:F], wg.rearrange("e (c p) f -> (e c) p f", p=P)[n]).then_inc(w_loaded[q], 16)
                    sp.dma_start(w_raw[:, q, F:2 * F], wu.rearrange("e (c p) f -> (e c) p f", p=P)[n]).then_inc(w_loaded[q], 16)
                    sp.dma_start(w_raw[:, q, 2 * F:CW], wd_quarters[n // DC, n % DC]).then_inc(w_loaded[q], 16)

                def step(n, q, first, last):
                    if not last:
                        load_x(n + 2, q)
                    load_w(n, q)
                    sp.wait_ge(s["res_used"], n + 1)
                    sp.dma_start(x_res[:, q], x2_rows[n]).then_inc(res_loaded[q], 16)
                    sp.wait_ge(s["xn_ready"], n + 1)
                    sp.dma_start(xn_rows[n], xn[:, q]).then_inc(xn_stored[q], 16)
                    sp.wait_ge(s["w_ready"], n + 1)
                    sp.dma_start(halves[n, 0], w_hi[:, q].bitcast(F32)).then_inc(s["w_stored"], 16)
                    sp.dma_start(halves[n, 1], w_lo[:, q].bitcast(F32)).then_inc(s["w_stored"], 16)
                    sp.wait_ge(s["w_stored"], n * 32 + 32)
                    if not first:
                        sp.wait_ge(s["acc_ready"], n)
                        sp.dma_start(out_rows[n - 1], acc[:, 1 - q]).then_inc(acc_stored[1 - q], 16)

                pipeline(sp, step)
                sp.wait_ge(s["acc_ready"], TILES)
                sp.dma_start(out_rows[TILES - 1], acc[:, 1]).then_inc(acc_stored[1], 16)
                sp.wait_ge(s["table_ready"], 1)
                sp.dma_start(tile_table.rearrange("(p w) -> p w", w=2), table[:]).then_inc(s["table_out"], 16)
                sp.wait_ge(s["table_out"], 16)
                sp.wait_ge(x_loaded[0], 8 * TILES + 16)
                for i in range(2):
                    sp.wait_ge(xn_stored[i], 8 * TILES + 16)
                    sp.wait_ge(acc_stored[i], 8 * TILES + 16)

            @block.gpsimd
            def _(pool):
                pool.sem_inc(s["w_used"], 2)
                pool.sem_inc(s["pair_used"], 2)
                nc.gpsimd.memset(half[:], -0.5).then_inc(s["half_ready"], 1)
                nc.gpsimd.memset(unused[:, :, 0], NO_TOKEN).then_inc(s["clear_ready"], 1)
                nc.gpsimd.memset(unused[:, :, 1], 0).then_inc(s["clear_ready"], 1)
                pool.wait_ge(s["half_ready"], 1)
                pool.wait_ge(s["slots_clear"], 16)

                def inverse_root(n, q):
                    pool.wait_ge(s["moments_ready"], n + 1)
                    nc.gpsimd.tensor_tensor(rstd[:, q:q + 1], moments[:, 1:2], half[:], ALU.pow).then_inc(s["rstd_ready"], 1)

                def scatter(n, q):
                    pool.wait_ge(s["pair_ready"], n + 1)
                    alone(pool, s["passed"])
                    for j in range(2):
                        pool.indirect_dma_start(out=pairs, out_offset=bass.IndirectOffsetOnAxis(ap=slot[:, q, j:j + 1], axis=0),
                                                in_=pair[:, q, j], in_offset=None).then_inc(scattered[q], 16)
                    pool.wait_ge(scattered[q], (n - q) * 16 + 32)
                    pool.sem_inc(s["pair_used"], 1)

                def step(n, q, first, last):
                    if first:
                        inverse_root(0, 0)
                    if not last:
                        inverse_root(n + 1, 1 - q)
                    pool.wait_ge(w_loaded[q], (n - q) * 24 + 48)
                    alone(pool, s["passed"])
                    nc.gpsimd.tensor_copy(w_hi[:, q], w_raw[:, q]).then_inc(s["pool_step"], 1)
                    pool.wait_ge(s["pool_step"], n + 1)
                    nc.gpsimd.tensor_tensor(w_lo[:, q], w_raw[:, q], w_hi[:, q].bitcast(F32), ALU.subtract).then_inc(s["w_ready"], 1)
                    pool.wait_ge(s["w_ready"], n + 1)
                    pool.sem_inc(s["w_used"], 1)
                    if not first:
                        scatter(n - 1, 1 - q)

                pipeline(pool, step)
                scatter(TILES - 1, 1)
                for i in range(2):
                    pool.wait_ge(scattered[i], 16 * TILES)

            @block.scalar
            def _(act):
                act.wait_ge(s["raw_in0"], 16)
                nc.scalar.activation(sg_hi[:], raw[:, 0], ACT.Copy).then_inc(s["rounded"], 1)
                act.wait_ge(s["raw_in1"], 16)
                nc.scalar.activation(su_hi[:], raw[:, 1], ACT.Copy).then_inc(s["rounded"], 1)
                act.wait_ge(s["raw_in2"], 16)
                nc.scalar.activation(sd_hi[:], raw[:, 0], ACT.Copy).then_inc(s["rounded"], 1)

                def x_high(n):
                    act.wait_ge(s["xT_filled"], n + 1)
                    nc.scalar.activation(xT_hi[:], psum[:, XT], ACT.Copy).then_inc(s["xT_rounded"], 1)

                def route(n):
                    act.wait_ge(s["gap_ready"], n + 1)
                    nc.scalar.activation(e_gap[:], gap[:], ACT.Exp).then_inc(s["e_gap_ready"], 1)

                def step(n, q, first, last):
                    if first:
                        x_high(0)
                    act.wait_ge(s["gate_filled"], n + 1)
                    nc.scalar.activation(act_half[:], psum[:, GATE], ACT.Tanh, scale=0.5).then_inc(s["squashed"], 1)
                    if not last:
                        x_high(n + 1)
                    act.wait_ge(s["hT_filled"], n + 1)
                    nc.scalar.activation(hT_hi[:], psum[:, HT], ACT.Copy).then_inc(s["hT_rounded"], 1)
                    route(n)

                pipeline(act, step)

            @block.tensor
            def _(pe):
                pe.wait_ge(s["consts_ready"], 1)
                pe.wait_ge(s["split"], 4)

                def x_transposes(n, q):
                    pe.wait_ge(s["xn_ready"], n + 1)
                    for c in range(DC):
                        last = nc.tensor.transpose(psum[:, XT, P * c:P * (c + 1)], xn[:, q, P * c:P * (c + 1)], ident[:])
                    last.then_inc(s["xT_filled"], 1)

                def product(out, left_hi, left_lo, right_hi, right_lo):
                    for c in range(DC):
                        lh, ll = (t[:, P * c:P * (c + 1)] for t in (left_hi, left_lo))
                        nc.tensor.matmul(out, lh, right_hi[:, c], start=(c == 0), stop=False)
                        nc.tensor.matmul(out, lh, right_lo[:, c], start=False, stop=False)
                        last = nc.tensor.matmul(out, ll, right_hi[:, c], start=False, stop=(c == DC - 1))
                    return last

                def down(n, q):
                    pe.wait_ge(s["hT_rounded"], n + 1)
                    pe.wait_ge(s["hT_split"], n + 1)
                    pe.wait_ge(s["res_used"], n + 1)
                    product(psum[:, DOWN + q], hT_hi, hT_lo, sd_hi, sd_lo).then_inc(s["down_filled"], 1)

                def rank(n):
                    pe.wait_ge(s["picked_ready"], n + 1)
                    nc.tensor.matmul(psum[:, RANK, 0:E], tri[:], picked[:], start=True, stop=False)
                    nc.tensor.matmul(psum[:, RANK, 0:E], ones[:], counted[:], start=False, stop=True).then_inc(s["rank_filled"], 1)

                def step(n, q, first, last):
                    if first:
                        x_transposes(0, 0)
                    pe.wait_ge(s["xT_rounded"], n + 1)
                    pe.wait_ge(s["xT_split"], n + 1)
                    product(psum[:, GATE], xT_hi, xT_lo, sg_hi, sg_lo).then_inc(s["gate_filled"], 1)
                    if not first:
                        rank(n - 1)
                    product(psum[:, UP], xT_hi, xT_lo, su_hi, su_lo).then_inc(s["up_filled"], 1)
                    product(psum[:, LOGITS, 0:E], xT_hi, xT_lo, wr_hi, wr_lo).then_inc(s["logits_filled"], 1)
                    if not first:
                        down(n - 1, 1 - q)
                    if not last:
                        x_transposes(n + 1, 1 - q)
                    pe.wait_ge(s["hidden_ready"], n + 1)
                    for c in range(DC):
                        mm = nc.tensor.transpose(psum[:, HT, P * c:P * (c + 1)], hidden[:, P * c:P * (c + 1)], ident[:])
                    mm.then_inc(s["hT_filled"], 1)

                pipeline(pe, step)
                rank(TILES - 1)
                down(TILES - 1, 1)
                pe.wait_ge(s["pair_ready"], TILES)
                nc.tensor.matmul(psum[:, RANK, 0:E], ones[:], counted[:], start=True, stop=True).then_inc(s["counts_filled"], 1)

            @block.vector
            def _(dve):
                dve.sem_inc(s["x_used"], 2)
                dve.sem_inc(s["res_used"], 2)
                dve.wait_ge(s["const_in"], 64)
                dve.wait_ge(s["bias_in"], 16)
                for lo, hi, at in ((sg_lo, sg_hi, 0), (su_lo, su_hi, 1), (sd_lo, sd_hi, 0)):
                    dve.wait_ge(s["rounded"], 1 + (0 if lo is sg_lo else 1 if lo is su_lo else 2))
                    nc.vector.tensor_tensor(lo[:], raw[:, at], hi[:].bitcast(F32), ALU.subtract).then_inc(s["split"], 1)
                count = [0]
                base = [0]

                def then(ins):
                    count[0] += 1
                    ins.then_inc(s["vec_step"], 1)
                    dve.wait_ge(s["vec_step"], base[0] + count[0])

                dve.wait_ge(s["wr_in"], 16)
                then(nc.vector.tensor_copy(wr_hi[:], wr_raw[:]))
                nc.vector.tensor_tensor(wr_lo[:], wr_raw[:], wr_hi[:].bitcast(F32), ALU.subtract).then_inc(s["split"], 1)
                nc.vector.memset(counted[:], 0.0)
                then(nc.vector.tensor_copy(token[:], columns[:, 0:1]))
                nc.vector.memset(best_f[:], 0.0).then_inc(s["consts_ready"], 1)

                def normalise(n, q):
                    dve.wait_ge(x_loaded[q], per_slot(n, q))
                    then(nc.vector.bn_stats(stats[:], x_in[:, q]))
                    alone(dve, s["passed"])
                    then(nc.vector.bn_aggr(moments[:], stats[:]))
                    nc.vector.tensor_scalar(moments[:, 1:2], moments[:, 1:2], EPS, None, ALU.add).then_inc(s["moments_ready"], 1)
                    dve.wait_ge(s["rstd_ready"], n + 1)
                    dve.wait_ge(xn_stored[q], per_slot(n, q))
                    nc.vector.tensor_scalar(xn[:, q], x_in[:, q], moments[:, 0:1], rstd[:, q:q + 1], ALU.subtract, ALU.mult).then_inc(s["xn_ready"], 1)
                    dve.wait_ge(s["xn_ready"], n + 1)
                    dve.sem_inc(s["x_used"], 1)

                def per_slot(n, q):
                    return (n - q) * 8 + 16

                def x_low(n):
                    dve.wait_ge(s["xT_rounded"], n + 1)
                    nc.vector.tensor_tensor(xT_lo[:], psum[:, XT], xT_hi[:].bitcast(F32), ALU.subtract).then_inc(s["xT_split"], 1)

                def add(n, q):
                    dve.wait_ge(s["down_filled"], n + 1)
                    dve.wait_ge(res_loaded[q], per_slot(n, q))
                    dve.wait_ge(acc_stored[q], per_slot(n, q))
                    nc.vector.tensor_tensor(acc[:, q], psum[:, DOWN + q], x_res[:, q], ALU.add).then_inc(s["acc_ready"], 1)
                    dve.wait_ge(s["acc_ready"], n + 1)
                    dve.sem_inc(s["res_used"], 1)

                def choose(n):
                    dve.wait_ge(s["logits_filled"], n + 1)
                    then(nc.vector.tensor_tensor(logits[:], psum[:, LOGITS, 0:E], router_bias[:], ALU.add))
                    alone(dve, s["passed"])
                    then(nc.vector.max(best[:], logits[:]))
                    nc.vector.tensor_tensor(gap[:], best[:, 1:2], best[:, 0:1], ALU.subtract).then_inc(s["gap_ready"], 1)
                    then(nc.vector.max_index(best_at[:], best[:], logits[:]))
                    then(nc.vector.tensor_copy(best_f[:], best_at[:, 0:2]))
                    nc.vector.tensor_scalar(chosen[:, 0], columns[:, 1:1 + E], best_f[:, 0:1], None, ALU.is_equal)
                    then(nc.vector.tensor_scalar(chosen[:, 1], columns[:, 1:1 + E], best_f[:, 1:2], None, ALU.is_equal))
                    nc.vector.tensor_tensor(picked[:], chosen[:, 0], chosen[:, 1], ALU.add).then_inc(s["picked_ready"], 1)

                def assign(n, q):
                    dve.wait_ge(s["e_gap_ready"], n + 1)
                    then(nc.vector.tensor_scalar(gate_sum[:], e_gap[:], 1.0, None, ALU.add))
                    then(nc.vector.reciprocal(gates[:, 0:1], gate_sum[:]))
                    then(nc.vector.tensor_tensor(gates[:, 1:2], gates[:, 0:1], e_gap[:], ALU.mult))
                    dve.wait_ge(s["rank_filled"], n + 1)
                    nc.vector.tensor_tensor_reduce(junk[:, 0], psum[:, RANK, 0:E], chosen[:, 0], 1.0, 0.0, ALU.mult, ALU.add, place[:, 0:1])
                    then(nc.vector.tensor_tensor_reduce(junk[:, 1], psum[:, RANK, 0:E], chosen[:, 1], 1.0, 0.0, ALU.mult, ALU.add, place[:, 1:2]))
                    then(nc.vector.scalar_tensor_tensor(slot_f[:], best_f[:], float(TOKENS), place[:], ALU.mult, ALU.add))
                    dve.wait_ge(s["pair_used"], n + 1)
                    nc.vector.tensor_copy(slot[:, q], slot_f[:])
                    nc.vector.tensor_copy(pair[:, q, :, 0], token[:].broadcast_to([P, 2]))
                    nc.vector.tensor_copy(pair[:, q, :, 1].bitcast(F32), gates[:])
                    then(nc.vector.tensor_tensor(counted[:], counted[:], picked[:], ALU.add))
                    nc.vector.tensor_scalar(token[:], token[:], float(P), None, ALU.add).then_inc(s["pair_ready"], 1)
                    dve.wait_ge(s["pair_ready"], n + 1)

                def step(n, q, first, last):
                    if first:
                        normalise(0, 0)
                        x_low(0)
                        normalise(1, 1)
                    if not first:
                        assign(n - 1, 1 - q)
                    dve.wait_ge(s["squashed"], n + 1)
                    then(nc.vector.scalar_tensor_tensor(act_half[:], act_half[:], 1.0, psum[:, GATE], ALU.add, ALU.mult))
                    dve.wait_ge(s["up_filled"], n + 1)
                    nc.vector.scalar_tensor_tensor(hidden[:], act_half[:], 0.5, psum[:, UP], ALU.mult, ALU.mult).then_inc(s["hidden_ready"], 1)
                    if not last:
                        x_low(n + 1)
                    choose(n)
                    dve.wait_ge(s["hT_rounded"], n + 1)
                    nc.vector.tensor_tensor(hT_lo[:], psum[:, HT], hT_hi[:].bitcast(F32), ALU.subtract).then_inc(s["hT_split"], 1)
                    if not first:
                        add(n - 1, 1 - q)

                step(0, 0, True, False)
                start = count[0]
                with dve.Fori(0, (TILES - 2) // 2) as i:
                    base[0], count[0] = i * ROUTE_STEPS + start, 0
                    normalise(2 * i + 2, 0)
                    step(2 * i + 1, 1, False, False)
                    normalise(2 * i + 3, 1)
                    step(2 * i + 2, 0, False, False)
                    assert count[0] == ROUTE_STEPS, count[0]
                base[0], count[0] = (TILES - 2) // 2 * ROUTE_STEPS + start, 0
                step(TILES - 1, 1, False, True)
                assign(TILES - 1, 1)
                add(TILES - 1, 1)

                dve.wait_ge(s["counts_filled"], 1)
                then(nc.vector.tensor_scalar(before[:, 0], psum[:, RANK, 0:E], float(P - 1), None, ALU.add))
                then(nc.vector.tensor_copy(counts_i[:, 0], before[:, 0]))
                then(nc.vector.tensor_scalar(counts_i[:, 1], counts_i[:, 0], P.bit_length() - 1, None, ALU.logical_shift_right))
                then(nc.vector.tensor_copy(n_tiles[:], counts_i[:, 1]))
                then(nc.vector.tensor_copy(ends[:, 0], n_tiles[:]))
                src = 0
                for shift in (1, 2, 4):
                    then(nc.vector.tensor_copy(ends[:, 1 - src, 0:shift], ends[:, src, 0:shift]))
                    then(nc.vector.tensor_tensor(ends[:, 1 - src, shift:E], ends[:, src, shift:E], ends[:, src, 0:E - shift], ALU.add))
                    src = 1 - src
                then(nc.vector.tensor_scalar(before[:, 0], ends[:, src], columns[:, 0:1], None, ALU.is_le))
                then(nc.vector.tensor_tensor_reduce(before[:, 1, 0:E - 1], before[:, 0, 0:E - 1], n_tiles[:, 0:E - 1], 1.0, 0.0, ALU.mult, ALU.add, table_f[:, 1:2]))
                then(nc.vector.tensor_reduce(table_f[:, 0:1], before[:, 0, 0:E - 1], mybir.AxisListType.X, ALU.add))
                then(nc.vector.tensor_tensor(table_f[:, 2:3], columns[:, 0:1], table_f[:, 1:2], ALU.subtract))
                then(nc.vector.tensor_scalar(table_f[:, 2:3], table_f[:, 2:3], float(P), None, ALU.mult))
                then(nc.vector.scalar_tensor_tensor(table_f[:, 1:2], table_f[:, 0:1], float(TOKENS), table_f[:, 2:3], ALU.mult, ALU.add))
                nc.vector.tensor_copy(table[:], table_f[:, 0:2]).then_inc(s["table_ready"], 1)


def experts_phase(nc, k, xn_rows, out, halves, pairs, tile_table):
    with ExitStack() as ctx:
        def sb(name, shape, dt=F32):
            return ctx.enter_context(nc.sbuf_tensor("e_" + name, shape, dt))

        def sem(name):
            return ctx.enter_context(nc.semaphore("e_" + name))

        CHUNKS = E * DC
        w_hi, w_lo = sb("w_hi", [P, CHUNKS, CW], F32R), sb("w_lo", [P, CHUNKS, CW], F32R)
        ident = sb("ident", [P, P])
        table = sb("table", [1, 2 * P], I32)
        pairs_sb = sb("pairs", [P, VISITS + 1, 2], I32)
        take, current = sb("take", [P, 2], I32), sb("current", [P, 2, 2], I32)
        x = sb("x", [P, 2, D])
        xT_hi, xT_lo = sb("xT_hi", [P, D], F32R), sb("xT_lo", [P, D], F32R)
        hidden = sb("hidden", [P, F])
        hT_hi, hT_lo = sb("hT_hi", [P, F], F32R), sb("hT_lo", [P, F], F32R)
        y = sb("y", [P, D])
        psum = ctx.enter_context(nc.psum_tensor("e_psum", [P, 8, 512], F32))
        XT, GATE_UP, HT, DOWN = 0, 1, 3, 4

        names = "const_in table_in w_in cleared pair_in take_ready current_ready x_used xT_filled xT_rounded xT_split gate_filled squashed vec_step "
        names += "hidden_ready hT_filled hT_rounded hT_split down_filled y_ready y_used added passed"
        s = {n: sem(n) for n in names.split()}
        x_in = [sem(f"x_in{i}") for i in range(2)]

        def pipeline(eng, step):
            step(0, 0, True, False)
            with eng.Fori(0, (VISITS - 2) // 2) as i:
                step(2 * i + 1, 1, False, False)
                step(2 * i + 2, 0, False, False)
            step(VISITS - 1, 1, False, True)

        def per_slot(n, q):
            return (n - q) * 8 + 16

        with nc.Block() as block:
            @block.sync
            def _(sp):
                sp.dma_start(ident[:], k["ident"]).then_inc(s["const_in"], 16)
                sp.dma_start(table[:], tile_table.rearrange("(a n) -> a n", a=1)).then_inc(s["table_in"], 16)
                sp.wait_ge(s["table_in"], 16)
                for e in range(E):
                    for i, w in enumerate((w_hi, w_lo)):
                        sp.dma_start(w[:, DC * e:DC * (e + 1)].bitcast(F32), halves[DC * e:DC * (e + 1), i].rearrange("c p n -> p c n")).then_inc(s["w_in"], 16)
                    with sp.Fori(VISITS // E * e, VISITS // E * (e + 1) + (e == E - 1)) as n:
                        row = sp.value_load(table[0:1, bass.ds(2 * n + 1, 1)], min_val=0, max_val=SLOTS - P)
                        sp.dma_start(pairs_sb[:, bass.ds(n, 1)], pairs[bass.ds(row, P)].unsqueeze(1)).then_inc(s["pair_in"], 16)
                        sp.wait_ge(s["pair_in"], 16 * n + 16)
                        alone(sp, s["passed"])
                    sp.wait_ge(s["w_in"], 32 * (e + 1))

            @block.gpsimd
            def _(pool):
                pool.wait_ge(s["cleared"], 1)

                def fetch(n, q):
                    pool.wait_ge(s["pair_in"], 16 * n + 16)
                    alone(pool, s["passed"])
                    pool.wait_ge(s["x_used"], n + 1)
                    alone(pool, s["passed"])
                    nc.gpsimd.tensor_copy(take[:, q:q + 1], pairs_sb[:, bass.ds(n, 1), 0]).then_inc(s["take_ready"], 1)
                    pool.wait_ge(s["take_ready"], n + 1)
                    alone(pool, s["passed"])
                    pool.indirect_dma_start(out=x[:, q], out_offset=None, in_=xn_rows, in_offset=bass.IndirectOffsetOnAxis(ap=take[:, q:q + 1], axis=0),
                                            bounds_check=TOKENS - 1, oob_is_err=False).then_inc(x_in[q], 16)

                def give(n, q):
                    pool.wait_ge(s["y_ready"], n + 2)
                    alone(pool, s["passed"])
                    pool.indirect_dma_start(out=out, out_offset=bass.IndirectOffsetOnAxis(ap=current[:, q, 0:1], axis=0), in_=y[:], in_offset=None,
                                            bounds_check=TOKENS - 1, oob_is_err=False, compute_op=ALU.add).then_inc(s["added"], 16)
                    pool.wait_ge(s["added"], 16 * n + 16)
                    pool.sem_inc(s["y_used"], 1)
                    alone(pool, s["passed"])

                def step(n, q, first, last):
                    if first:
                        fetch(0, 0)
                        fetch(1, 1)
                    if not last:
                        fetch(n + 2, q)
                    nc.gpsimd.tensor_copy(current[:, q], pairs_sb[:, bass.ds(n, 1)].rearrange("p a w -> p (a w)")).then_inc(s["current_ready"], 1)
                    if not first:
                        give(n - 1, 1 - q)

                pool.sem_inc(s["y_used"], 1)
                pipeline(pool, step)
                give(VISITS - 1, 1)
                pool.wait_ge(x_in[0], per_slot(VISITS, 0))

            @block.scalar
            def _(act):
                act.sem_inc(s["y_ready"], 1)

                def x_high(n):
                    act.wait_ge(s["xT_filled"], n + 1)
                    nc.scalar.activation(xT_hi[:], psum[:, XT], ACT.Copy).then_inc(s["xT_rounded"], 1)

                def weigh(n, q):
                    act.wait_ge(s["down_filled"], n + 1)
                    act.wait_ge(s["current_ready"], n + 1)
                    act.wait_ge(s["y_used"], n + 1)
                    nc.scalar.activation(y[:], psum[:, DOWN], ACT.Copy, scale=current[:, q, 1:2].bitcast(F32)).then_inc(s["y_ready"], 1)

                def step(n, q, first, last):
                    if first:
                        x_high(0)
                    act.wait_ge(s["gate_filled"], n + 1)
                    nc.scalar.activation(hidden[:], psum[:, GATE_UP, 0:F], ACT.Tanh, scale=0.5).then_inc(s["squashed"], 1)
                    if not first:
                        weigh(n - 1, 1 - q)
                    if not last:
                        x_high(n + 1)
                    act.wait_ge(s["hT_filled"], n + 1)
                    nc.scalar.activation(hT_hi[:], psum[:, HT, 0:F], ACT.Copy).then_inc(s["hT_rounded"], 1)

                pipeline(act, step)
                weigh(VISITS - 1, 1)

            @block.tensor
            def _(pe):
                pe.wait_ge(s["const_in"], 16)
                pe.wait_ge(s["table_in"], 16)

                def x_transposes(n, q):
                    pe.wait_ge(x_in[q], per_slot(n, q))
                    for c in range(DC):
                        last = nc.tensor.transpose(psum[:, XT, P * c:P * (c + 1)], x[:, q, P * c:P * (c + 1)], ident[:])
                    last.then_inc(s["xT_filled"], 1)

                def expert_of(n):
                    return pe.value_load(table[0:1, bass.ds(2 * n, 1)], min_val=0, max_val=E - 1)

                def three(out, lh, ll, rh, rl, start, stop):
                    nc.tensor.matmul(out, lh, rh, start=start, stop=False)
                    nc.tensor.matmul(out, lh, rl, start=False, stop=False)
                    return nc.tensor.matmul(out, ll, rh, start=False, stop=stop)

                def down(n, e):
                    pe.wait_ge(s["hT_rounded"], n + 1)
                    pe.wait_ge(s["hT_split"], n + 1)
                    pe.wait_ge(s["y_ready"], n + 1)
                    for j in range(FC):
                        at = bass.ds(DC * e + FC * j, FC)
                        last = three(psum[:, DOWN], hT_hi[:, P * j:P * (j + 1)], hT_lo[:, P * j:P * (j + 1)],
                                     w_hi[:, at, 2 * F:CW], w_lo[:, at, 2 * F:CW], j == 0, j == FC - 1)
                    last.then_inc(s["down_filled"], 1)

                def step(n, q, first, last):
                    if first:
                        x_transposes(0, 0)
                    e = expert_of(n)
                    pe.wait_ge(s["w_in"], 32 * e + 32)
                    pe.wait_ge(s["xT_rounded"], n + 1)
                    pe.wait_ge(s["xT_split"], n + 1)
                    for c in range(DC):
                        at = bass.ds(DC * e + c, 1)
                        mm = three(psum[:, GATE_UP], xT_hi[:, P * c:P * (c + 1)], xT_lo[:, P * c:P * (c + 1)],
                                   w_hi[:, at, 0:2 * F], w_lo[:, at, 0:2 * F], c == 0, c == DC - 1)
                    mm.then_inc(s["gate_filled"], 1)
                    if not first:
                        down(n - 1, expert_of(n - 1))
                    if not last:
                        x_transposes(n + 1, 1 - q)
                    pe.wait_ge(s["hidden_ready"], n + 1)
                    for j in range(FC):
                        mm = nc.tensor.transpose(psum[:, HT, P * j:P * (j + 1)], hidden[:, j:F:FC], ident[:])
                    mm.then_inc(s["hT_filled"], 1)

                pipeline(pe, step)
                down(VISITS - 1, expert_of(VISITS - 1))

            @block.vector
            def _(dve):
                nc.vector.memset(x[:], 0.0).then_inc(s["cleared"], 1)
                dve.sem_inc(s["x_used"], 2)

                def x_low(n):
                    dve.wait_ge(s["xT_rounded"], n + 1)
                    dve.sem_inc(s["x_used"], 1)
                    nc.vector.tensor_tensor(xT_lo[:], psum[:, XT], xT_hi[:].bitcast(F32), ALU.subtract).then_inc(s["xT_split"], 1)

                def step(n, q, first, last):
                    if first:
                        x_low(0)
                    dve.wait_ge(s["squashed"], n + 1)
                    nc.vector.scalar_tensor_tensor(hidden[:], hidden[:], 1.0, psum[:, GATE_UP, 0:F], ALU.add, ALU.mult).then_inc(s["vec_step"], 1)
                    dve.wait_ge(s["vec_step"], n + 1)
                    nc.vector.scalar_tensor_tensor(hidden[:], hidden[:], 0.5, psum[:, GATE_UP, F:2 * F], ALU.mult, ALU.mult).then_inc(s["hidden_ready"], 1)
                    if not last:
                        x_low(n + 1)
                    dve.wait_ge(s["hT_rounded"], n + 1)
                    nc.vector.tensor_tensor(hT_lo[:], psum[:, HT, 0:F], hT_hi[:].bitcast(F32), ALU.subtract).then_inc(s["hT_split"], 1)

                pipeline(dve, step)


VEC_STEPS = 32
ROUTE_STEPS = 28


def build(nc, x, ctx, mask, wq, wk, wv, wo, wr, wg, wu, wd, sg, su, sd, expert_bias, out):
    def scratch(name, shape, dt=F32):
        return nc.dram_tensor(name, shape, dt, kind="Internal").ap()

    def tiles(rows):
        return rows.rearrange("(t p) d -> t p d", p=P)

    x2, xn = scratch("x2_rows", (TOKENS, D)), scratch("xn_rows", (TOKENS, D))
    halves = scratch("w_halves", (E * DC, 2, P, CW))
    pairs, tile_table = scratch("pairs", (SLOTS, 2), I32), scratch("tile_table", (2 * P,), I32)
    out_rows = out.rearrange("b l d -> (b l) d")
    k = tables(nc)
    attention_phase(nc, k, tiles(x.rearrange("b l d -> (b l) d")), tiles(ctx.rearrange("b l d -> (b l) d")), mask, wq, wk, wv, wo, tiles(x2))
    shared_phase(nc, k, tiles(x2), tiles(xn), tiles(out_rows), wr, sg, su, sd, expert_bias, wg, wu, wd, pairs, halves, tile_table)
    experts_phase(nc, k, xn, out_rows, halves, pairs, tile_table)


_INS = ["x", "ctx_1024", "mask_1x1xSxS2_ik0"] + [f"L0_xattn_{n}" for n in ("wq", "wk", "wv", "wo")]
_INS += [f"L0_ffn_{n}" for n in ("Wr", "Wg", "Wu", "Wd", "Sg", "Su", "Sd", "expert_bias")]


def kernel(**inputs):
    import numpy as _np
    import concourse.bacc as _bacc
    from concourse import mybir as _mybir
    from concourse.bass_utils import run_bass_kernel_spmd as _run

    nc = _bacc.Bacc("TRN2", target_bir_lowering=False, num_devices=1)
    arrays, args = {}, []
    for name in _INS:
        a = _np.ascontiguousarray(inputs[name])
        arrays[f"in_{name}"] = a
        args.append(nc.dram_tensor(f"in_{name}", a.shape, _mybir.dt.from_np(a.dtype), kind="ExternalInput").ap())
    out = nc.dram_tensor("out_0", (B, L, D), _mybir.dt.float32, kind="ExternalOutput").ap()
    build(nc, *args, out)
    return _run(nc, [arrays], core_ids=[0]).results[0]["out_0"]
```

```python
import math
from contextlib import ExitStack

import numpy as np
import concourse.bass as bass
from concourse import mybir

F32, F32R, I32, U32 = mybir.dt.float32, mybir.dt.float32r, mybir.dt.int32, mybir.dt.uint32
ALU = mybir.AluOpType
ACT = mybir.ActivationFunctionType

P = 128
B, L, D = 8, 512, 512
TOKENS = B * L
TILES = TOKENS // P
TT = L // P
DC = D // P
H, KVH, DK = 16, 2, 32
REP = H // KVH
KV = KVH * DK
GH = P // DK
HG = H // GH
RING = GH + 2
E, F, FS = 8, 256, 512
FC = F // P
CW = 2 * F + D // FC
VISITS = TOKENS * 2 // P + E
SLOTS = E * TOKENS + (VISITS + 1) * P
NO_TOKEN = 1 << 20
EPS = 1e-5
MASKED = 2.0 ** 100
HUGE = 3.0e38



def alone(eng, passed):
    eng.sem_inc(passed, 1)


def tables(nc):
    pos = np.arange(L, dtype=np.float32)
    inv_freq = (1.0 / 10000.0 ** (np.arange(0, DK, 2, dtype=np.float32) / DK)).astype(np.float32)
    freqs = pos[:, None] * inv_freq[None, :]
    cos, sin = np.cos(freqs), np.sin(freqs)
    rope = np.stack([np.concatenate([cos, cos], 1), np.concatenate([-sin, sin], 1)], 1).astype(np.float32)
    rope = np.ascontiguousarray(rope.reshape(TT, P, 2, DK).transpose(1, 0, 2, 3))
    pick = np.zeros((2 * GH, P), np.float32)
    for r in range(2 * GH):
        pick[r, DK * (r % GH):DK * (r % GH + 1)] = 1.0
    def constant(name, array):
        return nc.inline_tensor(array.astype(np.float32), name=name).ap()

    return dict(
        ident=constant("c_ident", np.eye(P)),
        pick=constant("c_pick", pick),
        ones=constant("c_ones", np.ones((P, P))),
        tri=constant("c_tri", np.triu(np.ones((P, P)), 1)),
        columns=constant("c_columns", np.concatenate([np.arange(P)[:, None], np.tile(np.arange(E), (P, 1))], 1)),
        rope_k=constant("c_rope_k", rope),
        rope_q=constant("c_rope_q", -rope / math.sqrt(DK)),
    )


def attention_phase(nc, k, x_rows, ctx_rows, mask, wq, wk, wv, wo, x2_rows):
    with ExitStack() as ctx:
        def sb(name, shape, dt=F32):
            return ctx.enter_context(nc.sbuf_tensor("a_" + name, shape, dt))

        ident = sb("ident", [P, P])
        ident_r = sb("ident_r", [P, P], F32R)
        pick_raw = sb("pick_raw", [2 * GH, P])
        pick = sb("pick", [2 * GH, P], F32R)
        half = sb("half", [P, 1])
        rope_q = sb("rope_q", [P, TT, 2, DK])
        rope_k = sb("rope_k", [P, TT, 2, DK])
        bias = sb("bias", [P, TT, L])
        wq_hi, wq_lo = sb("wq_hi", [P, DC, D], F32R), sb("wq_lo", [P, DC, D], F32R)
        wo_hi, wo_lo = sb("wo_hi", [P, DC, D], F32R), sb("wo_lo", [P, DC, D], F32R)
        wkv = sb("wkv", [P, DC, 2 * KV])
        x_in, ctx_in, x_res = sb("x_in", [P, 2, D]), sb("ctx_in", [P, 2, D]), sb("x_res", [P, 2, D])
        x2 = sb("x2", [P, 2, D])
        stats, moments, rstd = sb("stats", [P, 6]), sb("moments", [P, 2]), sb("rstd", [P, 1])
        xn = sb("xn", [P, D])
        xT_hi, xT_lo = sb("xT_hi", [P, 2, D], F32R), sb("xT_lo", [P, 2, D], F32R)
        ctxT = sb("ctxT", [P, 2, D])
        q_cos, q_sin = sb("q_cos", [P, D]), sb("q_sin", [P, D])
        k_cos, k_sin, k_rot = sb("k_cos", [P, KV]), sb("k_sin", [P, KV]), sb("k_rot", [P, KV])
        q = sb("q", [P, 2, TT, D])
        q_stack = sb("q_stack", [P, 2, TT, 4, DK], F32R)
        k_stack = sb("k_stack", [P, 2, KVH, 4, DK], F32R)
        qT = sb("qT", [P, 2, L], F32R)
        kT = sb("kT", [P, 2, KVH, L], F32R)
        v = sb("v", [P, 2, TT, KV])
        low = sb("low", [P, H, TT])
        total = sb("total", [P, 2, TT, GH])
        inverse = sb("inverse", [P, TT, GH])
        inverse_hl = sb("inverse_hl", [P, TT, 2, GH], F32R)
        inverseT = sb("inverseT", [2 * GH, L], F32R)
        spread = sb("spread", [P, L])
        probs = sb("probs", [P, 2, TT, L])
        probsT = sb("probsT", [P, RING, TT, L])
        att = sb("att", [P, L])
        attT_hi, attT_lo = sb("attT_hi", [P, HG, L], F32R), sb("attT_lo", [P, HG, L], F32R)
        psum = ctx.enter_context(nc.psum_tensor("a_psum", [P, 8, 512], F32))

        names = "const_in kv_in wq_in wo_in mask_in wq_rounded wo_rounded weights_split consts_ready half_ready bias_ready ctx_used "
        names += "stats_ready aggregated moments_ready rstd_ready xn_ready xT_rounded "
        names += "xT_filled xT_split ctxT_filled ctxT_ready q_filled q_rotated kv_filled kv_read kT_filled kT_ready "
        names += "qT_filled qT_ready inverse_filled inverseT_ready spread_filled spread_ready wo_filled x2_ready "
        names += "q_added k_added k_rounded k_split k_ready stack_rounded stack_ready "
        names += "s_filled low_ready probs_ready t_filled t_freed_act t_freed_vec inverted inverse_rounded inverse_ready out_filled "
        names += "att_ready att_rounded att_split passed"
        s = {n: ctx.enter_context(nc.semaphore("a_" + n)) for n in names.split()}
        x_loaded, ctx_loaded, res_loaded, stored = (
            [ctx.enter_context(nc.semaphore(f"a_{n}{i}")) for i in range(2)] for n in ("x_in", "ctx_in", "x_res", "stored"))

        STATS, XN, XT, Q, KT, WO = ({slot: t for t, slot in enumerate(slots)} for slots in (
            (3, 4, 7, 8), (4, 5, 8, 9), (5, 6, 9, 10), (6, 7, 10, 11), (8, 9, 12, 13), (2, 3, 4, 5)))

        OUT_BANK = 5

        def t_bank(h, c):
            return 2 + (TT * h + c + (h == H - 1)) % 3

        def evacuated_by_act(h, c):
            return c % 2 == 0

        def evacuated(n, act):
            return sum(evacuated_by_act(i // TT, i % TT) == act for i in range(n))

        ET, VT = evacuated(H * TT, True), evacuated(H * TT, False)

        def ring(h):
            return h % GH + (GH * (h // GH % 2) if h % GH < 2 else 0)

        def weigh_steps(part, h):
            g = h // GH - 1
            if g == -1:
                return [(g, c) for c in range(TT)] if h == 0 and part != "first" else [None] * TT
            return {0: [None, (g, 0), None, (g, 1)], 1: [None, (g, 2), None, (g, 3)]}.get(h % GH, [None] * TT)

        def scale_slot(part, h):
            if h == 1 and part != "first":
                return -1
            return h // GH - 1 if h % GH == 2 and h > GH else None

        def turns(first, last):
            order = []
            for h in range(H):
                if h % GH == 0 and not (first and h == 0):
                    order.append(("inverse", h // GH - 1))
                if h in XT and not last:
                    order += [("xT", XT[h]), ("ctxT", XT[h])]
                if h % GH == 1 and not (first and h == 1):
                    order.append(("spread", h // GH - 1))
                if h in WO and not first:
                    order.append(("wo", WO[h]))
                if h in Q and not last:
                    order += [("kv", Q[h]), ("q", Q[h])]
                if h + 3 < H or not last:
                    order.append(("qT", h + 3))
                if h in KT and not last:
                    order.append(("kT", KT[h]))
            return order

        start = [("xT", 0), ("ctxT", 0)]
        for t in range(TT):
            start += [("kv", t), ("q", t)]
            if t + 1 < TT:
                start += [("xT", t + 1), ("ctxT", t + 1)]
            start += [("kT", t)]
        start += [("qT", H), ("qT", H + 1), ("qT", H + 2)]
        orders = {"start": start, "first": turns(True, False), "middle": turns(False, False), "last": turns(False, True),
                  "end": [("inverse", -1), ("spread", -1)] + [("wo", t) for t in range(TT)]}
        before = {"first": "start", "middle": "middle", "last": "middle", "end": "last"}
        assert len(orders["middle"]) % 2 == 0 and orders["first"][-2:] == orders["middle"][-2:]
        bank_of_first = {"middle": 0, "last": 0, "first": len(orders["first"]) % 2, "end": len(orders["last"]) % 2}
        bank_of_first["start"] = (bank_of_first["first"] + len(start)) % 2

        def bank(part, kind, i):
            return psum[:, 6 + (bank_of_first[part] + orders[part].index((kind, i))) % 2, :]

        KINDS = {"xT": (TT, 1, "xT_split"), "ctxT": (TT, 1, "ctxT_ready"), "q": (TT, 1, "q_rotated"), "kv": (TT, 1, "kv_read"),
                 "kT": (TT, 1, "kT_ready"), "qT": (H, 0, "qT_ready"), "inverse": (HG, 0, "inverseT_ready"),
                 "spread": (HG, 0, "spread_ready"), "wo": (TT, -1, "x2_ready")}

        def upto(b, kind, i):
            per, ahead, _ = KINDS[kind]
            return b * per + (ahead * per + i + 1)

        def wait_count(eng, signal, count):
            if not isinstance(count, int) or count > 0:
                eng.wait_ge(signal, count)

        def bodies(eng, body):
            body("start", -1, 1)
            body("first", 0, 0)
            with eng.Fori(0, (B - 2) // 2) as i:
                body("middle", 2 * i + 1, 1)
                body("middle", 2 * i + 2, 0)
            body("last", B - 1, 1)
            body("end", B, 0)

        with nc.Block() as block:
            @block.sync
            def _(sp):
                for i in range(2):
                    sp.sem_inc(stored[i], 16)

                def load_tile(b, t):
                    wait_count(sp, s["xn_ready"], b * TT + (TT + t - 1))
                    sp.dma_start(x_in[:, t % 2], x_rows[b * TT + (TT + t)]).then_inc(x_loaded[t % 2], 16)
                    wait_count(sp, s["ctx_used"], b * TT + (TT + t - 1))
                    sp.dma_start(ctx_in[:, t % 2], ctx_rows[b * TT + (TT + t)]).then_inc(ctx_loaded[t % 2], 16)

                def load_residual(b, t):
                    sp.dma_start(x_res[:, t % 2], x_rows[b * TT + (t - TT)]).then_inc(res_loaded[t % 2], 16)

                def store(b, t):
                    sp.wait_ge(s["x2_ready"], b * TT + (t - TT + 1))
                    sp.dma_start(x2_rows[b * TT + (t - TT)], x2[:, t % 2]).then_inc(stored[t % 2], 16)

                def body(part, b, par):
                    if part == "start":
                        for dst, src in ((ident, k["ident"]), (pick_raw, k["pick"]), (rope_q, k["rope_q"]), (rope_k, k["rope_k"])):
                            sp.dma_start(dst[:], src).then_inc(s["const_in"], 16)
                        load_tile(b, 0)
                        sp.dma_start(probs[:, 0], wq.rearrange("(c p) n -> p c n", p=P)).then_inc(s["wq_in"], 16)
                        sp.dma_start(wkv[:, :, 0:KV], wk.rearrange("(c p) n -> p c n", p=P)).then_inc(s["kv_in"], 16)
                        sp.dma_start(wkv[:, :, KV:2 * KV], wv.rearrange("(c p) n -> p c n", p=P)).then_inc(s["kv_in"], 16)
                        load_tile(b, 1)
                        sp.dma_start(probsT[:, 0].bitcast(I32), mask.rearrange("a b (t p) k -> p (a b t) k", p=P)).then_inc(s["mask_in"], 16)
                        sp.dma_start(probs[:, 1], wo.rearrange("(c p) n -> p c n", p=P)).then_inc(s["wo_in"], 16)
                        load_tile(b, 2)
                        load_tile(b, 3)
                        return
                    if part != "first":
                        load_residual(b, 0)
                        load_residual(b, 1)
                    if part in ("first", "middle"):
                        load_tile(b, 0)
                        load_tile(b, 1)
                    if part != "first":
                        for t in range(TT):
                            store(b, t)
                            if t + 2 < TT:
                                load_residual(b, t + 2)
                    if part in ("first", "middle"):
                        load_tile(b, 2)
                        load_tile(b, 3)

                bodies(sp, body)
                for i in range(2):
                    sp.wait_ge(stored[i], 16 + 16 * B * TT // 2)

            @block.gpsimd
            def _(pool):
                def inverse_root(b, t):
                    pool.wait_ge(s["moments_ready"], upto(b, "xT", t))
                    nc.gpsimd.tensor_tensor(rstd[:], moments[:, 1:2], half[:], ALU.pow).then_inc(s["rstd_ready"], 1)

                def finish_projection(b, par, t):
                    n = upto(b, "q", t)
                    pool.wait_ge(s["kv_read"], n)
                    nc.gpsimd.tensor_tensor(k_rot[:], k_cos[:], k_sin[:], ALU.add).then_inc(s["k_added"], 1)
                    kr = k_rot[:].rearrange("p (h d) -> p h d", h=KVH)
                    pool.wait_ge(s["k_added"], n)
                    alone(pool, s["passed"])
                    wait_count(pool, s["kT_ready"], n - 2)
                    alone(pool, s["passed"])
                    nc.gpsimd.tensor_copy(k_stack[:, t % 2, :, 0], kr).then_inc(s["k_rounded"], 1)
                    pool.wait_ge(s["k_rounded"], n)
                    nc.gpsimd.tensor_tensor(k_stack[:, t % 2, :, 1], kr, k_stack[:, t % 2, :, 0].bitcast(F32), ALU.subtract).then_inc(s["k_split"], 1)
                    pool.wait_ge(s["k_split"], n)
                    alone(pool, s["passed"])
                    nc.gpsimd.tensor_copy(k_stack[:, t % 2, :, 2:4], k_stack[:, t % 2, :, 0:2].bitcast(F32)).then_inc(s["k_ready"], 1)
                    pool.wait_ge(s["q_rotated"], n)
                    nc.gpsimd.tensor_tensor(q[:, 1 - par, t], q_cos[:], q_sin[:], ALU.add).then_inc(s["q_added"], 1)

                def stack(b, par, h):
                    batch, at = (par, h) if h < H else (1 - par, h - H)
                    twice_q = q[:, batch, :, DK * at:DK * (at + 1)].unsqueeze(2).broadcast_to([P, TT, 2, DK])
                    if h == H:
                        pool.wait_ge(s["q_added"], upto(b, "q", TT - 1))
                        alone(pool, s["passed"])
                    wait_count(pool, s["qT_filled"], upto(b, "qT", h - 2))
                    alone(pool, s["passed"])
                    nc.gpsimd.tensor_copy(q_stack[:, h % 2, :, 0:2], twice_q).then_inc(s["stack_rounded"], 1)
                    pool.wait_ge(s["stack_rounded"], upto(b, "qT", h))
                    nc.gpsimd.tensor_tensor(q_stack[:, h % 2, :, 2:4], twice_q, q_stack[:, h % 2, :, 0:2].bitcast(F32), ALU.subtract).then_inc(s["stack_ready"], 1)

                def output_low(b, g):
                    pool.wait_ge(s["att_rounded"], upto(b, "spread", g))
                    nc.gpsimd.tensor_tensor(attT_lo[:, g % HG], att[:], attT_hi[:, g % HG].bitcast(F32), ALU.subtract).then_inc(s["att_split"], 1)

                def body(part, b, par):
                    if part == "start":
                        nc.gpsimd.memset(half[:], -0.5).then_inc(s["half_ready"], 1)
                        pool.wait_ge(s["half_ready"], 1)
                        inverse_root(b, 0)
                        inverse_root(b, 1)
                        for t in range(TT):
                            finish_projection(b, par, t)
                            if t + 2 < TT:
                                inverse_root(b, t + 2)
                        for h in range(H, H + 4):
                            stack(b, par, h)
                        return
                    if part == "end":
                        output_low(b, -1)
                        return
                    for h in range(H):
                        if h - 1 in Q and part != "last":
                            finish_projection(b, par, Q[h - 1])
                        if h + 4 < H or part != "last":
                            stack(b, par, h + 4)
                        if scale_slot(part, h) is not None:
                            output_low(b, scale_slot(part, h))
                        if h in STATS and part != "last":
                            inverse_root(b, STATS[h])

                bodies(pool, body)

            @block.scalar
            def _(act):
                def turned_x(part, b, t):
                    act.wait_ge(s["xT_filled"], upto(b, "xT", t))
                    nc.scalar.activation(xT_hi[:, t % 2], bank(part, "xT", t), ACT.Copy).then_inc(s["xT_rounded"], 1)

                def turned_ctx(part, b, t):
                    act.wait_ge(s["ctxT_filled"], upto(b, "ctxT", t))
                    act.sem_inc(s["ctx_used"], 1)
                    nc.scalar.activation(ctxT[:, t % 2], bank(part, "ctxT", t), ACT.Copy).then_inc(s["ctxT_ready"], 1)

                def turned_q(part, b, h):
                    act.wait_ge(s["qT_filled"], upto(b, "qT", h))
                    wait_count(act, s["s_filled"], b * (H * TT) + TT * (h - 1))
                    nc.scalar.activation(qT[:, h % 2], bank(part, "qT", h), ACT.Copy).then_inc(s["qT_ready"], 1)

                def exp(b, h, t):
                    act.wait_ge(s["low_ready"], b * (H * TT) + (TT * h + t + 1))
                    if h % GH == 0 and t == 0:
                        wait_count(act, s["inverse_ready"], b * HG + (h // GH - 1))
                    nc.scalar.activation(probs[:, h % 2, t], probs[:, h % 2, t], ACT.Exp, bias=low[:, h % H, t:t + 1], scale=-1.0,
                                         accum_out=total[:, h // GH % 2, t, h % GH:h % GH + 1]).then_inc(s["probs_ready"], 1)

                def evacuate(b, h, c):
                    if evacuated_by_act(h, c):
                        act.wait_ge(s["t_filled"], b * (H * TT) + (TT * h + c + 1))
                        nc.scalar.activation(probsT[:, ring(h), c], psum[:, t_bank(h, c)], ACT.Copy).then_inc(s["t_freed_act"], 1)

                def turned_inverse(part, b, g):
                    act.wait_ge(s["inverse_filled"], upto(b, "inverse", g))
                    nc.scalar.activation(inverseT[:], bank(part, "inverse", g)[0:2 * GH], ACT.Copy).then_inc(s["inverseT_ready"], 1)

                def copy_spread(part, b, g):
                    act.wait_ge(s["spread_filled"], upto(b, "spread", g))
                    wait_count(act, s["att_ready"], upto(b, "spread", g - 1))
                    nc.scalar.activation(spread[:], bank(part, "spread", g), ACT.Copy).then_inc(s["spread_ready"], 1)

                def output_high(part, b, g):
                    act.wait_ge(s["att_ready"], upto(b, "spread", g))
                    if g == 0 and part != "first":
                        act.wait_ge(s["wo_filled"], upto(b, "wo", TT - 1))
                    nc.scalar.activation(attT_hi[:, g % HG], att[:], ACT.Copy).then_inc(s["att_rounded"], 1)

                def body(part, b, par):
                    if part == "start":
                        act.wait_ge(s["wq_in"], 16)
                        nc.scalar.activation(wq_hi[:], probs[:, 0], ACT.Copy).then_inc(s["wq_rounded"], 1)
                        turned_x(part, b, 0)
                        turned_ctx(part, b, 0)
                        act.wait_ge(s["wo_in"], 16)
                        nc.scalar.activation(wo_hi[:], probs[:, 1], ACT.Copy).then_inc(s["wo_rounded"], 1)
                        for t in range(1, TT):
                            turned_x(part, b, t)
                            turned_ctx(part, b, t)
                        turned_q(part, b, H)
                        turned_q(part, b, H + 1)
                        for t in range(TT):
                            exp(b, H, t)
                        turned_q(part, b, H + 2)
                        exp(b, H + 1, 0)
                        exp(b, H + 1, 1)
                        return
                    if part == "end":
                        turned_inverse(part, b, -1)
                        copy_spread(part, b, -1)
                        output_high(part, b, -1)
                        return
                    for h in range(H):
                        evacuate(b, h, 0)
                        if h in XT and part != "last":
                            turned_x(part, b, XT[h])
                        if h + 1 < H or part != "last":
                            exp(b, h + 1, 2)
                        if h in XT and part != "last":
                            turned_ctx(part, b, XT[h])
                        if h + 1 < H or part != "last":
                            exp(b, h + 1, 3)
                        if h % GH == 0 and not (part == "first" and h == 0):
                            turned_inverse(part, b, h // GH - 1)
                        if h % GH == 1 and not (part == "first" and h == 1):
                            copy_spread(part, b, h // GH - 1)
                        if scale_slot(part, h) is not None:
                            output_high(part, b, scale_slot(part, h))
                        evacuate(b, h, 2)
                        if h + 3 < H or part != "last":
                            turned_q(part, b, h + 3)
                        if h + 2 < H or part != "last":
                            exp(b, h + 2, 0)
                            exp(b, h + 2, 1)

                bodies(act, body)

            @block.tensor
            def _(pe):
                pe.wait_ge(s["consts_ready"], 2)
                pe.wait_ge(s["kv_in"], 32)

                def turn(part, b, kind, i):
                    at = orders[part].index((kind, i)) - 2
                    if at >= 0:
                        kind_was, was = orders[part][at]
                        pe.wait_ge(s[KINDS[kind_was][2]], upto(b, kind_was, was))
                    elif part != "start":
                        kind_was, was = orders[before[part]][at]
                        pe.wait_ge(s[KINDS[kind_was][2]], upto(b, kind_was, was) - KINDS[kind_was][0])
                    return bank(part, kind, i)

                def four(out, src, identity):
                    for i in range(4):
                        last = nc.tensor.transpose(out[:, P * i:P * (i + 1)], src(i), identity[:])
                    return last

                def product(out, left_hi, left_lo, right_hi, right_lo, c):
                    nc.tensor.matmul(out, left_hi, right_hi[:, c], start=(c == 0), stop=False)
                    nc.tensor.matmul(out, left_hi, right_lo[:, c], start=False, stop=False)
                    return nc.tensor.matmul(out, left_lo, right_hi[:, c], start=False, stop=(c == DC - 1))

                def turn_x(part, b, t):
                    pe.wait_ge(s["xn_ready"], upto(b, "xT", t))
                    four(turn(part, b, "xT", t), lambda i: xn[:, P * i:P * (i + 1)], ident).then_inc(s["xT_filled"], 1)

                def turn_ctx(part, b, t):
                    pe.wait_ge(ctx_loaded[t % 2], b * 32 + (48 + 16 * (t // 2)))
                    four(turn(part, b, "ctxT", t), lambda i: ctx_in[:, t % 2, P * i:P * (i + 1)], ident).then_inc(s["ctxT_filled"], 1)

                def project_kv(part, b, t):
                    pe.wait_ge(s["ctxT_ready"], upto(b, "ctxT", t))
                    out = turn(part, b, "kv", t)[:, 0:2 * KV]
                    for c in range(DC):
                        last = nc.tensor.matmul(out, ctxT[:, t % 2, P * c:P * (c + 1)], wkv[:, c], start=(c == 0), stop=(c == DC - 1))
                    last.then_inc(s["kv_filled"], 1)

                def project_q(part, b, t, c):
                    if c == 0:
                        pe.wait_ge(s["xT_rounded"], upto(b, "xT", t))
                        pe.wait_ge(s["xT_split"], upto(b, "xT", t))
                        turn(part, b, "q", t)
                    last = product(bank(part, "q", t), xT_hi[:, t % 2, P * c:P * (c + 1)], xT_lo[:, t % 2, P * c:P * (c + 1)], wq_hi, wq_lo, c)
                    if c == DC - 1:
                        last.then_inc(s["q_filled"], 1)

                def turn_k(part, b, t):
                    pe.wait_ge(s["k_ready"], upto(b, "kT", t))
                    out = turn(part, b, "kT", t)
                    for i in range(KVH):
                        last = nc.tensor.transpose(out[:, P * i:P * (i + 1)].bitcast(F32R), k_stack[:, t % 2, i].rearrange("p r d -> p (r d)"), ident_r[:])
                    last.then_inc(s["kT_filled"], 1)

                def turn_q(part, b, h):
                    pe.wait_ge(s["stack_ready"], upto(b, "qT", h))
                    four(turn(part, b, "qT", h).bitcast(F32R), lambda i: q_stack[:, h % 2, i].rearrange("p r d -> p (r d)"),
                         ident_r).then_inc(s["qT_filled"], 1)

                def scores(part, b, par, h, t):
                    batch, at = (par, h) if h < H else (1 - par, h - H)
                    if t == 0:
                        pe.wait_ge(s["qT_ready"], upto(b, "qT", h))
                        if at == 0:
                            pe.wait_ge(s["kT_ready"], upto(b, "kT", TT - 1))
                    wait_count(pe, s["low_ready"], b * (H * TT) + (TT * h + t - 1))
                    nc.tensor.matmul(psum[:, t % 2], qT[:, h % 2, P * t:P * (t + 1)], kT[:, batch, at // REP], start=True, stop=True).then_inc(s["s_filled"], 1)

                def turn_probs(part, b, h, c):
                    if c == 0:
                        pe.wait_ge(s["probs_ready"], b * (H * TT) + (TT * h + TT))
                    i = TT * h + c - 1
                    while t_bank(i // TT % H, i % TT) != t_bank(h, c):
                        i -= 1
                    if i >= 0 or part != "first":
                        back, i = (0, i) if i >= 0 else (1, i + H * TT)
                        if evacuated_by_act(i // TT, i % TT):
                            pe.wait_ge(s["t_freed_act"], b * ET + (evacuated(i + 1, True) - back * ET))
                        else:
                            pe.wait_ge(s["t_freed_vec"], b * VT + (evacuated(i + 1, False) - back * VT))
                    four(psum[:, t_bank(h, c)], lambda t: probs[:, h % 2, t, P * c:P * (c + 1)], ident).then_inc(s["t_filled"], 1)

                def weighted(b, par, g, c):
                    if c == 0:
                        pe.wait_ge(s["t_freed_act"], b * ET + evacuated(TT * GH * (g + 1), True))
                        pe.wait_ge(s["t_freed_vec"], b * VT + evacuated(TT * GH * (g + 1), False))
                        wait_count(pe, s["att_ready"], upto(b, "spread", g - 1))
                    batch, at = (par, g) if g >= 0 else (1 - par, g + HG)
                    for j in range(GH):
                        h = GH * at + j
                        last = nc.tensor.matmul(psum[DK * j:DK * (j + 1), OUT_BANK], v[:, batch, c, DK * (h // REP):DK * (h // REP + 1)],
                                                probsT[:, ring(h), c], start=(c == 0), stop=(c == TT - 1))
                    if c == TT - 1:
                        last.then_inc(s["out_filled"], 1)

                def turn_inverse(part, b, g):
                    pe.wait_ge(s["inverse_ready"], upto(b, "inverse", g))
                    out = turn(part, b, "inverse", g)
                    for t in range(TT):
                        last = nc.tensor.transpose(out[0:2 * GH, P * t:P * (t + 1)].bitcast(F32R), inverse_hl[:, t].rearrange("p r h -> p (r h)"), ident_r[:])
                    last.then_inc(s["inverse_filled"], 1)

                def spread_inverse(part, b, g):
                    pe.wait_ge(s["inverseT_ready"], upto(b, "inverse", g))
                    nc.tensor.matmul(turn(part, b, "spread", g), pick[:], inverseT[:], start=True, stop=True).then_inc(s["spread_filled"], 1)

                def project_out(part, b, t, c):
                    if c == 0:
                        pe.wait_ge(s["weights_split"], 2)
                        pe.wait_ge(s["att_split"], upto(b, "spread", -1))
                        turn(part, b, "wo", t)
                    last = product(bank(part, "wo", t), attT_hi[:, c, P * t:P * (t + 1)], attT_lo[:, c, P * t:P * (t + 1)], wo_hi, wo_lo, c)
                    if c == DC - 1:
                        last.then_inc(s["wo_filled"], 1)

                def body(part, b, par):
                    if part == "start":
                        turn_x(part, b, 0)
                        turn_ctx(part, b, 0)
                        pe.wait_ge(s["weights_split"], 1)
                        for t in range(TT):
                            project_kv(part, b, t)
                            for c in range(DC):
                                project_q(part, b, t, c)
                            if t + 1 < TT:
                                turn_x(part, b, t + 1)
                                turn_ctx(part, b, t + 1)
                            turn_k(part, b, t)
                        turn_q(part, b, H)
                        turn_q(part, b, H + 1)
                        for t in range(TT):
                            scores(part, b, par, H, t)
                        turn_q(part, b, H + 2)
                        scores(part, b, par, H + 1, 0)
                        scores(part, b, par, H + 1, 1)
                        return
                    if part == "end":
                        turn_inverse(part, b, -1)
                        spread_inverse(part, b, -1)
                        for c in range(TT):
                            weighted(b, par, -1, c)
                        for t in range(TT):
                            for c in range(DC):
                                project_out(part, b, t, c)
                        return
                    for h in range(H):
                        def beside(c):
                            if h in WO and part != "first":
                                project_out(part, b, WO[h], c)
                            if h in Q and part != "last":
                                if c == 0:
                                    project_kv(part, b, Q[h])
                                project_q(part, b, Q[h], c)
                            if weigh_steps(part, h)[c]:
                                weighted(b, par, *weigh_steps(part, h)[c])

                        turn_probs(part, b, h, 0)
                        if h + 1 < H or part != "last":
                            scores(part, b, par, h + 1, 2)
                        if h in XT and part != "last":
                            turn_x(part, b, XT[h])
                            turn_ctx(part, b, XT[h])
                        turn_probs(part, b, h, 1)
                        if h % GH == 0 and not (part == "first" and h == 0):
                            turn_inverse(part, b, h // GH - 1)
                        if h + 1 < H or part != "last":
                            scores(part, b, par, h + 1, 3)
                        if h % GH == 1 and not (part == "first" and h == 1):
                            spread_inverse(part, b, h // GH - 1)
                        beside(0)
                        turn_probs(part, b, h, 2)
                        turn_probs(part, b, h, 3)
                        beside(1)
                        if h + 3 < H or part != "last":
                            turn_q(part, b, h + 3)
                        if h in KT and part != "last":
                            turn_k(part, b, KT[h])
                        if h + 2 < H or part != "last":
                            scores(part, b, par, h + 2, 0)
                        beside(2)
                        if h + 2 < H or part != "last":
                            scores(part, b, par, h + 2, 1)
                        beside(3)

                bodies(pe, body)

            @block.vector
            def _(dve):
                def moments_of(b, t):
                    n = upto(b, "xT", t)
                    dve.wait_ge(x_loaded[t % 2], b * 32 + (48 + 16 * (t // 2)))
                    nc.vector.bn_stats(stats[:], x_in[:, t % 2]).then_inc(s["stats_ready"], 1)
                    dve.wait_ge(s["stats_ready"], n)
                    alone(dve, s["passed"])
                    wait_count(dve, s["xn_ready"], n - 1)
                    alone(dve, s["passed"])
                    nc.vector.bn_aggr(moments[:], stats[:]).then_inc(s["aggregated"], 1)
                    dve.wait_ge(s["aggregated"], n)
                    nc.vector.tensor_scalar(moments[:, 1:2], moments[:, 1:2], EPS, None, ALU.add).then_inc(s["moments_ready"], 1)

                def normalise(b, t):
                    n = upto(b, "xT", t)
                    dve.wait_ge(s["rstd_ready"], n)
                    wait_count(dve, s["xT_rounded"], n - 1)
                    nc.vector.tensor_scalar(xn[:], x_in[:, t % 2], moments[:, 0:1], rstd[:, 0:1], ALU.subtract, ALU.mult).then_inc(s["xn_ready"], 1)

                def x_low(part, b, t):
                    dve.wait_ge(s["xT_rounded"], upto(b, "xT", t))
                    nc.vector.tensor_tensor(xT_lo[:, t % 2], bank(part, "xT", t), xT_hi[:, t % 2].bitcast(F32), ALU.subtract).then_inc(s["xT_split"], 1)

                def rotate(src, table, t, heads, cos_part, sin_part):
                    halves = src.rearrange("p (h r d) -> p h r d", h=heads, r=2)
                    cos = table[:, t, 0].unsqueeze(1).broadcast_to([P, heads, DK])
                    sin = table[:, t, 1].rearrange("p (r d) -> p r d", r=2)
                    nc.vector.tensor_tensor(cos_part[:].rearrange("p (h d) -> p h d", h=heads), src.rearrange("p (h d) -> p h d", h=heads), cos, ALU.mult)
                    out = sin_part[:].rearrange("p (h r d) -> p h r d", h=heads, r=2)
                    nc.vector.tensor_tensor(out[:, :, 0], halves[:, :, 1], sin[:, 0].unsqueeze(1).broadcast_to([P, heads, DK // 2]), ALU.mult)
                    return nc.vector.tensor_tensor(out[:, :, 1], halves[:, :, 0], sin[:, 1].unsqueeze(1).broadcast_to([P, heads, DK // 2]), ALU.mult)

                def projected_kv(part, b, par, t):
                    n = upto(b, "kv", t)
                    dve.wait_ge(s["kv_filled"], n)
                    wait_count(dve, s["k_ready"], n - 1)
                    kv = bank(part, "kv", t)
                    rotate(kv[:, 0:KV], rope_k, t, KVH, k_cos, k_sin)
                    nc.vector.tensor_copy(v[:, 1 - par, t], kv[:, KV:2 * KV]).then_inc(s["kv_read"], 1)

                def projected_q(part, b, t):
                    n = upto(b, "q", t)
                    dve.wait_ge(s["q_filled"], n)
                    wait_count(dve, s["q_added"], n - 1)
                    rotate(bank(part, "q", t), rope_q, t, H, q_cos, q_sin).then_inc(s["q_rotated"], 1)

                def turned_k(part, b, par, t):
                    dve.wait_ge(s["kT_filled"], upto(b, "kT", t))
                    nc.vector.tensor_copy(kT[:, 1 - par, :, P * t:P * (t + 1)],
                                          bank(part, "kT", t)[:, 0:KVH * P].rearrange("p (h t) -> p h t", h=KVH)).then_inc(s["kT_ready"], 1)

                def lowest(b, h, t):
                    dve.wait_ge(s["s_filled"], b * (H * TT) + (TT * h + t + 1))
                    if t == 0:
                        wait_count(dve, s["t_filled"], b * (H * TT) + TT * (h - 1))
                    alone(dve, s["passed"])
                    nc.vector.tensor_tensor_reduce(probs[:, h % 2, t], psum[:, t % 2], bias[:, t], 1.0, HUGE, ALU.add, ALU.min,
                                                   low[:, h % H, t:t + 1]).then_inc(s["low_ready"], 1)

                def evacuate(b, h, c):
                    if not evacuated_by_act(h, c):
                        dve.wait_ge(s["t_filled"], b * (H * TT) + (TT * h + c + 1))
                        nc.vector.tensor_copy(probsT[:, ring(h), c], psum[:, t_bank(h, c)]).then_inc(s["t_freed_vec"], 1)

                def invert(b, g):
                    n = upto(b, "inverse", g)
                    dve.wait_ge(s["probs_ready"], b * (H * TT) + TT * GH * (g + 1))
                    nc.vector.reciprocal(inverse[:], total[:, g % 2]).then_inc(s["inverted"], 1)
                    dve.wait_ge(s["inverted"], n)
                    nc.vector.tensor_copy(inverse_hl[:, :, 0], inverse[:]).then_inc(s["inverse_rounded"], 1)
                    dve.wait_ge(s["inverse_rounded"], n)
                    nc.vector.tensor_tensor(inverse_hl[:, :, 1], inverse[:], inverse_hl[:, :, 0].bitcast(F32), ALU.subtract).then_inc(s["inverse_ready"], 1)

                def scale(b, g):
                    n = upto(b, "spread", g)
                    dve.wait_ge(s["spread_ready"], n)
                    dve.wait_ge(s["out_filled"], n)
                    wait_count(dve, s["att_split"], upto(b, "spread", g - 1))
                    nc.vector.tensor_tensor(att[:], psum[:, OUT_BANK], spread[:], ALU.mult).then_inc(s["att_ready"], 1)

                def add_residual(part, b, t):
                    dve.wait_ge(s["wo_filled"], upto(b, "wo", t))
                    dve.wait_ge(res_loaded[t % 2], b * 32 + (16 * (t // 2) - 16))
                    dve.wait_ge(stored[t % 2], b * 32 + (16 * (t // 2) - 16))
                    nc.vector.tensor_tensor(x2[:, t % 2], bank(part, "wo", t), x_res[:, t % 2], ALU.add).then_inc(s["x2_ready"], 1)

                def body(part, b, par):
                    if part == "start":
                        dve.wait_ge(s["const_in"], 64)
                        nc.vector.tensor_copy(ident_r[:], ident[:]).then_inc(s["consts_ready"], 1)
                        nc.vector.tensor_copy(pick[:], pick_raw[:]).then_inc(s["consts_ready"], 1)
                        moments_of(b, 0)
                        normalise(b, 0)
                        dve.wait_ge(s["wq_rounded"], 1)
                        nc.vector.tensor_tensor(wq_lo[:], probs[:, 0], wq_hi[:].bitcast(F32), ALU.subtract).then_inc(s["weights_split"], 1)
                        x_low(part, b, 0)
                        moments_of(b, 1)
                        normalise(b, 1)
                        for t in range(TT):
                            projected_kv(part, b, par, t)
                            if t == 0:
                                dve.wait_ge(s["wo_rounded"], 1)
                                nc.vector.tensor_tensor(wo_lo[:], probs[:, 1], wo_hi[:].bitcast(F32), ALU.subtract).then_inc(s["weights_split"], 1)
                                dve.wait_ge(s["mask_in"], 16)
                                nc.vector.tensor_scalar(bias[:], probsT[:, 0].bitcast(I32), 0.0, MASKED, ALU.is_equal, ALU.mult).then_inc(s["bias_ready"], 1)
                            projected_q(part, b, t)
                            if t + 1 < TT:
                                x_low(part, b, t + 1)
                            turned_k(part, b, par, t)
                            if t + 2 < TT:
                                moments_of(b, t + 2)
                                normalise(b, t + 2)
                        dve.wait_ge(s["bias_ready"], 1)
                        for t in range(TT):
                            lowest(b, H, t)
                        lowest(b, H + 1, 0)
                        lowest(b, H + 1, 1)
                        return
                    if part == "end":
                        scale(b, -1)
                        for t in range(TT):
                            add_residual(part, b, t)
                        return
                    for h in range(H):
                        if h - 1 in WO and part != "first":
                            add_residual(part, b, WO[h - 1])
                        if h - 1 in Q and part != "last":
                            projected_q(part, b, Q[h - 1])
                        if h + 1 < H or part != "last":
                            lowest(b, h + 1, 2)
                        if h in XT and part != "last":
                            x_low(part, b, XT[h])
                        if h + 1 < H or part != "last":
                            lowest(b, h + 1, 3)
                        evacuate(b, h, 1)
                        if h in Q and part != "last":
                            projected_kv(part, b, par, Q[h])
                        if h % GH == GH - 1:
                            invert(b, h // GH)
                        if scale_slot(part, h) is not None:
                            scale(b, scale_slot(part, h))
                        evacuate(b, h, 3)
                        if h in KT and part != "last":
                            turned_k(part, b, par, KT[h])
                        if h + 2 < H or part != "last":
                            lowest(b, h + 2, 0)
                            lowest(b, h + 2, 1)
                        if h in XN and part != "last":
                            normalise(b, XN[h])
                        if h in STATS and part != "last":
                            moments_of(b, STATS[h])

                bodies(dve, body)


def shared_phase(nc, k, x2_rows, xn_rows, out_rows, wr, sg, su, sd, expert_bias, wg, wu, wd, pairs, halves, tile_table):
    with ExitStack() as ctx:
        def sb(name, shape, dt=F32):
            return ctx.enter_context(nc.sbuf_tensor("b_" + name, shape, dt))

        def sem(name):
            return ctx.enter_context(nc.semaphore("b_" + name))

        ident, tri, ones = sb("ident", [P, P]), sb("tri", [P, P]), sb("ones", [P, P])
        columns = sb("columns", [P, 1 + E])
        half = sb("half", [P, 1])
        raw = sb("raw", [P, 3, DC, D])
        sg_hi, sg_lo = sb("sg_hi", [P, DC, D], F32R), sb("sg_lo", [P, DC, D], F32R)
        su_hi, su_lo = sb("su_hi", [P, DC, D], F32R), sb("su_lo", [P, DC, D], F32R)
        sd_hi, sd_lo = sb("sd_hi", [P, DC, D], F32R), sb("sd_lo", [P, DC, D], F32R)
        router = sb("router", [P, DC, E])
        router_bias = sb("router_bias", [P, E])
        unused = sb("unused", [P, SLOTS // P, 2], I32)
        x_in, x_res, acc = sb("x_in", [P, 2, D]), sb("x_res", [P, 2, D]), sb("acc", [P, 2, D])
        stats, moments, rstd = sb("stats", [P, 6]), sb("moments", [P, 2]), sb("rstd", [P, 2])
        xn = sb("xn", [P, 2, D])
        xT_hi, xT_lo = sb("xT_hi", [P, D], F32R), sb("xT_lo", [P, D], F32R)
        xT = sb("xT", [P, D])
        act_half, hidden = sb("act_half", [P, FS]), sb("hidden", [P, FS])
        hT_hi, hT_lo = sb("hT_hi", [P, FS], F32R), sb("hT_lo", [P, FS], F32R)
        w_raw, w_hi, w_lo = sb("w_raw", [P, 2, CW]), sb("w_hi", [P, 2, CW], F32R), sb("w_lo", [P, 2, CW], F32R)
        logits, best, best_at, best_f = sb("logits", [P, E]), sb("best", [P, E]), sb("best_at", [P, E], U32), sb("best_f", [P, 2])
        chosen, picked, counted = sb("chosen", [P, 2, E]), sb("picked", [P, E]), sb("counted", [P, E])
        junk = sb("junk", [P, 2, E])
        gap, e_gap, gate_sum, gates, place = sb("gap", [P, 1]), sb("e_gap", [P, 1]), sb("gate_sum", [P, 1]), sb("gates", [P, 2]), sb("place", [P, 2])
        token = sb("token", [P, 1])
        slot_f, slot, pair = sb("slot_f", [P, 2]), sb("slot", [P, 2, 2], I32), sb("pair", [P, 2, 2, 2], I32)
        counts_i, n_tiles, ends, table_f, table = sb("counts_i", [P, 2, E], I32), sb("n_tiles", [P, E]), sb("ends", [P, 2, E]), sb("table_f", [P, 4]), sb("table", [P, 2], I32)
        before = sb("before", [P, 2, E])
        psum = ctx.enter_context(nc.psum_tensor("b_psum", [P, 8, 512], F32))
        XT, GATE, UP, DOWN, HT, LOGITS, RANK = 0, 1, 2, 3, 5, 6, 7

        names = "const_in ident_in consts_ready half_ready raw_in0 raw_in1 raw_in2 wr_in rounded split slots_clear clear_ready bias_in "
        names += "x_used res_used moments_ready rstd_ready xn_ready xT_filled xT_copied xT_rounded xT_split gate_filled up_filled "
        names += "squashed gated hidden_ready hT_filled hT_rounded hT_split down_filled acc_ready logits_filled "
        names += "logits_ready picked_ready rank_filled gap_ready e_gap_ready pair_ready w_used w_ready w_stored table_ready table_out counts_filled "
        names += "vec_step pool_step passed pair_used"
        s = {n: sem(n) for n in names.split()}
        x_loaded, res_loaded, xn_stored, acc_stored, w_loaded, scattered = (
            [sem(f"{n}{i}") for i in range(2)] for n in ("x_in", "x_res", "xn_stored", "acc_stored", "w_in", "scattered"))

        def pipeline(eng, step):
            step(0, 0, True, False)
            with eng.Fori(0, (TILES - 2) // 2) as i:
                step(2 * i + 1, 1, False, False)
                step(2 * i + 2, 0, False, False)
            step(TILES - 1, 1, False, True)

        with nc.Block() as block:
            @block.sync
            def _(sp):
                for i in range(2):
                    sp.sem_inc(xn_stored[i], 16)
                    sp.sem_inc(acc_stored[i], 16)

                def load_x(n, q):
                    sp.wait_ge(s["x_used"], n + 1)
                    sp.dma_start(x_in[:, q], x2_rows[n % TILES]).then_inc(x_loaded[q], 16)

                load_x(0, 0)
                sp.dma_start(ident[:], k["ident"]).then_inc(s["ident_in"], 16)
                sp.dma_start(raw[:, 0], sg.rearrange("(c p) n -> p c n", p=P)).then_inc(s["raw_in0"], 16)
                for dst, src in ((tri, k["tri"]), (ones, k["ones"]), (columns, k["columns"])):
                    sp.dma_start(dst[:], src).then_inc(s["const_in"], 16)
                sp.dma_start(router[:], wr.rearrange("(c p) n -> p c n", p=P)).then_inc(s["wr_in"], 16)
                sp.dma_start(router_bias[:], expert_bias.rearrange("(a e) -> a e", a=1).broadcast_to([P, E])).then_inc(s["bias_in"], 16)
                sp.dma_start(raw[:, 1], su.rearrange("(c p) n -> p c n", p=P)).then_inc(s["raw_in1"], 16)
                load_x(1, 1)
                sp.dma_start(raw[:, 2], sd.rearrange("(c p) n -> p c n", p=P)).then_inc(s["raw_in2"], 16)
                sp.wait_ge(s["clear_ready"], 2)
                sp.dma_start(pairs.rearrange("(p s) w -> p s w", p=P), unused[:]).then_inc(s["slots_clear"], 16)

                wd_quarters = wd.rearrange("e f d -> e (f d)").rearrange("e (p c d) -> e c p d", p=P, c=DC)

                def load_w(n, q):
                    sp.wait_ge(s["w_used"], n + 1)
                    sp.dma_start(w_raw[:, q, 0:F], wg.rearrange("e (c p) f -> (e c) p f", p=P)[n]).then_inc(w_loaded[q], 16)
                    sp.dma_start(w_raw[:, q, F:2 * F], wu.rearrange("e (c p) f -> (e c) p f", p=P)[n]).then_inc(w_loaded[q], 16)
                    sp.dma_start(w_raw[:, q, 2 * F:CW], wd_quarters[n // DC, n % DC]).then_inc(w_loaded[q], 16)

                def step(n, q, first, last):
                    if first:
                        load_w(0, 0)
                    else:
                        sp.wait_ge(s["w_stored"], n * 32)
                        alone(sp, s["passed"])
                    if not last:
                        load_x(n + 2, q)
                        load_w(n + 1, 1 - q)
                    sp.wait_ge(s["res_used"], n + 1)
                    sp.dma_start(x_res[:, q], x2_rows[n]).then_inc(res_loaded[q], 16)
                    sp.wait_ge(s["xn_ready"], n + 1)
                    sp.dma_start(xn_rows[n], xn[:, q]).then_inc(xn_stored[q], 16)
                    sp.wait_ge(s["w_ready"], n + 1)
                    sp.dma_start(halves[n, 0], w_hi[:, q].bitcast(F32)).then_inc(s["w_stored"], 16)
                    sp.dma_start(halves[n, 1], w_lo[:, q].bitcast(F32)).then_inc(s["w_stored"], 16)
                    if not first:
                        sp.wait_ge(s["acc_ready"], n)
                        sp.dma_start(out_rows[n - 1], acc[:, 1 - q]).then_inc(acc_stored[1 - q], 16)

                pipeline(sp, step)
                sp.wait_ge(s["acc_ready"], TILES)
                sp.dma_start(out_rows[TILES - 1], acc[:, 1]).then_inc(acc_stored[1], 16)
                sp.wait_ge(s["table_ready"], 1)
                sp.dma_start(tile_table.rearrange("(p w) -> p w", w=2), table[:]).then_inc(s["table_out"], 16)
                sp.wait_ge(s["table_out"], 16)
                sp.wait_ge(x_loaded[0], 8 * TILES + 16)
                sp.wait_ge(s["w_stored"], 32 * TILES)
                for i in range(2):
                    sp.wait_ge(xn_stored[i], 8 * TILES + 16)
                    sp.wait_ge(acc_stored[i], 8 * TILES + 16)

            @block.gpsimd
            def _(pool):
                pool.sem_inc(s["w_used"], 2)
                pool.sem_inc(s["pair_used"], 2)
                nc.gpsimd.memset(half[:], -0.5).then_inc(s["half_ready"], 1)
                nc.gpsimd.memset(unused[:, :, 0], NO_TOKEN).then_inc(s["clear_ready"], 1)
                nc.gpsimd.memset(unused[:, :, 1], 0).then_inc(s["clear_ready"], 1)
                pool.wait_ge(s["half_ready"], 1)

                def inverse_root(n, q):
                    pool.wait_ge(s["moments_ready"], n + 1)
                    nc.gpsimd.tensor_tensor(rstd[:, q:q + 1], moments[:, 1:2], half[:], ALU.pow).then_inc(s["rstd_ready"], 1)

                def scatter(n, q, first=False):
                    pool.wait_ge(s["pair_ready"], n + 1)
                    alone(pool, s["passed"])
                    for j in range(2):
                        pool.indirect_dma_start(out=pairs, out_offset=bass.IndirectOffsetOnAxis(ap=slot[:, q, j:j + 1], axis=0),
                                                in_=pair[:, q, j], in_offset=None).then_inc(scattered[q], 16)
                    if not first:
                        pool.wait_ge(scattered[1 - q], (n - 1 - (1 - q)) * 16 + 32)
                        pool.sem_inc(s["pair_used"], 1)

                def step(n, q, first=False, last=False):
                    if first:
                        inverse_root(0, 0)
                    if not last:
                        inverse_root(n + 1, 1 - q)
                    pool.wait_ge(w_loaded[q], (n - q) * 24 + 48)
                    alone(pool, s["passed"])
                    nc.gpsimd.tensor_copy(w_hi[:, q], w_raw[:, q]).then_inc(s["pool_step"], 1)
                    pool.wait_ge(s["pool_step"], n + 1)
                    nc.gpsimd.tensor_tensor(w_lo[:, q], w_raw[:, q], w_hi[:, q].bitcast(F32), ALU.subtract).then_inc(s["w_ready"], 1)
                    pool.wait_ge(s["w_ready"], n + 1)
                    pool.sem_inc(s["w_used"], 1)

                step(0, 0, first=True)
                pool.wait_ge(s["slots_clear"], 16)
                step(1, 1)
                scatter(0, 0, first=True)
                with pool.Fori(0, (TILES - 2) // 2) as i:
                    step(2 * i + 2, 0)
                    scatter(2 * i + 1, 1)
                    step(2 * i + 3, 1)
                    scatter(2 * i + 2, 0)
                scatter(TILES - 1, 1)
                for i in range(2):
                    pool.wait_ge(scattered[i], 16 * TILES)

            @block.scalar
            def _(act):
                def x_high(n):
                    act.wait_ge(s["xT_filled"], n + 1)
                    nc.scalar.activation(xT[:], psum[:, XT], ACT.Copy).then_inc(s["xT_copied"], 1)
                    act.wait_ge(s["xT_copied"], n + 1)
                    nc.scalar.activation(xT_hi[:], xT[:], ACT.Copy).then_inc(s["xT_rounded"], 1)

                def round_weights(hi, at):
                    act.wait_ge(s[f"raw_in{at}"], 16)
                    nc.scalar.activation(hi[:], raw[:, at], ACT.Copy).then_inc(s["rounded"], 1)

                def hidden_high(n):
                    act.wait_ge(s["hT_filled"], n + 1)
                    nc.scalar.activation(hT_hi[:], psum[:, HT], ACT.Copy).then_inc(s["hT_rounded"], 1)

                def route(n):
                    act.wait_ge(s["gap_ready"], n + 1)
                    nc.scalar.activation(e_gap[:], gap[:], ACT.Exp).then_inc(s["e_gap_ready"], 1)

                def step(n, q, first, last):
                    if first:
                        round_weights(sg_hi, 0)
                        x_high(0)
                        round_weights(su_hi, 1)
                        round_weights(sd_hi, 2)
                    else:
                        hidden_high(n - 1)
                    act.wait_ge(s["gate_filled"], n + 1)
                    nc.scalar.activation(act_half[:], psum[:, GATE], ACT.Tanh, scale=0.5).then_inc(s["squashed"], 1)
                    if not last:
                        x_high(n + 1)
                    route(n)

                pipeline(act, step)
                hidden_high(TILES - 1)

            @block.tensor
            def _(pe):
                pe.wait_ge(s["ident_in"], 16)

                def x_transposes(n, q):
                    pe.wait_ge(s["xn_ready"], n + 1)
                    if not isinstance(n, int) or n > 0:
                        pe.wait_ge(s["xT_copied"], n)
                    for c in range(DC):
                        last = nc.tensor.transpose(psum[:, XT, P * c:P * (c + 1)], xn[:, q, P * c:P * (c + 1)], ident[:])
                    last.then_inc(s["xT_filled"], 1)

                def product(out, left_hi, left_lo, right_hi, right_lo):
                    for c in range(DC):
                        lh, ll = (t[:, P * c:P * (c + 1)] for t in (left_hi, left_lo))
                        nc.tensor.matmul(out, lh, right_hi[:, c], start=(c == 0), stop=False)
                        nc.tensor.matmul(out, lh, right_lo[:, c], start=False, stop=False)
                        last = nc.tensor.matmul(out, ll, right_hi[:, c], start=False, stop=(c == DC - 1))
                    return last

                def down(n, q):
                    pe.wait_ge(s["hT_rounded"], n + 1)
                    pe.wait_ge(s["hT_split"], n + 1)
                    pe.wait_ge(s["res_used"], n + 1)
                    product(psum[:, DOWN + q], hT_hi, hT_lo, sd_hi, sd_lo).then_inc(s["down_filled"], 1)

                def rank(n):
                    pe.wait_ge(s["picked_ready"], n + 1)
                    nc.tensor.matmul(psum[:, RANK, 0:E], tri[:], picked[:], start=True, stop=False)
                    nc.tensor.matmul(psum[:, RANK, 0:E], ones[:], counted[:], start=False, stop=True).then_inc(s["rank_filled"], 1)

                def step(n, q, first, last):
                    if first:
                        x_transposes(0, 0)
                        pe.wait_ge(s["split"], 1)
                    else:
                        rank(n - 1)
                    pe.wait_ge(s["xT_rounded"], n + 1)
                    pe.wait_ge(s["xT_split"], n + 1)
                    product(psum[:, GATE], xT_hi, xT_lo, sg_hi, sg_lo).then_inc(s["gate_filled"], 1)
                    if first:
                        pe.wait_ge(s["consts_ready"], 1)
                        pe.wait_ge(s["split"], 3)
                        pe.wait_ge(s["wr_in"], 16)
                    product(psum[:, UP], xT_hi, xT_lo, su_hi, su_lo).then_inc(s["up_filled"], 1)
                    pe.wait_ge(s["xT_copied"], n + 1)
                    for c in range(DC):
                        mm = nc.tensor.matmul(psum[:, LOGITS, 0:E], xT[:, P * c:P * (c + 1)], router[:, c], start=(c == 0), stop=(c == DC - 1))
                    mm.then_inc(s["logits_filled"], 1)
                    if not last:
                        x_transposes(n + 1, 1 - q)
                    if not first:
                        down(n - 1, 1 - q)
                    pe.wait_ge(s["hidden_ready"], n + 1)
                    for c in range(DC):
                        mm = nc.tensor.transpose(psum[:, HT, P * c:P * (c + 1)], hidden[:, P * c:P * (c + 1)], ident[:])
                    mm.then_inc(s["hT_filled"], 1)

                pipeline(pe, step)
                rank(TILES - 1)
                down(TILES - 1, 1)
                pe.wait_ge(s["pair_ready"], TILES)
                nc.tensor.matmul(psum[:, RANK, 0:E], ones[:], counted[:], start=True, stop=True).then_inc(s["counts_filled"], 1)

            @block.vector
            def _(dve):
                dve.sem_inc(s["x_used"], 2)
                dve.sem_inc(s["res_used"], 2)
                count = [0]
                base = [0]

                def then(ins):
                    count[0] += 1
                    ins.then_inc(s["vec_step"], 1)
                    dve.wait_ge(s["vec_step"], base[0] + count[0])

                def moments_of(n, q):
                    dve.wait_ge(x_loaded[q], per_slot(n, q))
                    then(nc.vector.bn_stats(stats[:], x_in[:, q]))
                    alone(dve, s["passed"])
                    then(nc.vector.bn_aggr(moments[:], stats[:]))
                    nc.vector.tensor_scalar(moments[:, 1:2], moments[:, 1:2], EPS, None, ALU.add).then_inc(s["moments_ready"], 1)

                def normalise(n, q):
                    dve.wait_ge(s["rstd_ready"], n + 1)
                    dve.wait_ge(xn_stored[q], per_slot(n, q))
                    nc.vector.tensor_scalar(xn[:, q], x_in[:, q], moments[:, 0:1], rstd[:, q:q + 1], ALU.subtract, ALU.mult).then_inc(s["xn_ready"], 1)
                    dve.wait_ge(s["xn_ready"], n + 1)
                    dve.sem_inc(s["x_used"], 1)

                def split_weights(lo, hi, at):
                    dve.wait_ge(s["rounded"], at + 1)
                    nc.vector.tensor_tensor(lo[:], raw[:, at], hi[:].bitcast(F32), ALU.subtract).then_inc(s["split"], 1)

                def per_slot(n, q):
                    return (n - q) * 8 + 16

                def x_low(n):
                    dve.wait_ge(s["xT_rounded"], n + 1)
                    nc.vector.tensor_tensor(xT_lo[:], xT[:], xT_hi[:].bitcast(F32), ALU.subtract).then_inc(s["xT_split"], 1)

                def hidden_low(n):
                    dve.wait_ge(s["hT_rounded"], n + 1)
                    nc.vector.tensor_tensor(hT_lo[:], psum[:, HT], hT_hi[:].bitcast(F32), ALU.subtract).then_inc(s["hT_split"], 1)

                def add(n, q):
                    dve.wait_ge(s["down_filled"], n + 1)
                    dve.wait_ge(res_loaded[q], per_slot(n, q))
                    dve.wait_ge(acc_stored[q], per_slot(n, q))
                    nc.vector.tensor_tensor(acc[:, q], psum[:, DOWN + q], x_res[:, q], ALU.add).then_inc(s["acc_ready"], 1)
                    dve.wait_ge(s["acc_ready"], n + 1)
                    dve.sem_inc(s["res_used"], 1)

                def choose(n):
                    dve.wait_ge(s["logits_filled"], n + 1)
                    then(nc.vector.tensor_tensor(logits[:], psum[:, LOGITS, 0:E], router_bias[:], ALU.add))
                    alone(dve, s["passed"])
                    then(nc.vector.max(best[:], logits[:]))
                    nc.vector.tensor_tensor(gap[:], best[:, 1:2], best[:, 0:1], ALU.subtract).then_inc(s["gap_ready"], 1)
                    then(nc.vector.max_index(best_at[:], best[:], logits[:]))
                    then(nc.vector.tensor_copy(best_f[:], best_at[:, 0:2]))
                    nc.vector.tensor_scalar(chosen[:, 0], columns[:, 1:1 + E], best_f[:, 0:1], None, ALU.is_equal)
                    then(nc.vector.tensor_scalar(chosen[:, 1], columns[:, 1:1 + E], best_f[:, 1:2], None, ALU.is_equal))
                    nc.vector.tensor_tensor(picked[:], chosen[:, 0], chosen[:, 1], ALU.add).then_inc(s["picked_ready"], 1)

                def assign(n, q):
                    dve.wait_ge(s["e_gap_ready"], n + 1)
                    then(nc.vector.tensor_scalar(gate_sum[:], e_gap[:], 1.0, None, ALU.add))
                    then(nc.vector.reciprocal(gates[:, 0:1], gate_sum[:]))
                    then(nc.vector.tensor_tensor(gates[:, 1:2], gates[:, 0:1], e_gap[:], ALU.mult))
                    dve.wait_ge(s["rank_filled"], n + 1)
                    nc.vector.tensor_tensor_reduce(junk[:, 0], psum[:, RANK, 0:E], chosen[:, 0], 1.0, 0.0, ALU.mult, ALU.add, place[:, 0:1])
                    then(nc.vector.tensor_tensor_reduce(junk[:, 1], psum[:, RANK, 0:E], chosen[:, 1], 1.0, 0.0, ALU.mult, ALU.add, place[:, 1:2]))
                    then(nc.vector.scalar_tensor_tensor(slot_f[:], best_f[:], float(TOKENS), place[:], ALU.mult, ALU.add))
                    dve.wait_ge(s["pair_used"], n + 1)
                    nc.vector.tensor_copy(slot[:, q], slot_f[:])
                    nc.vector.tensor_copy(pair[:, q, :, 0], token[:].broadcast_to([P, 2]))
                    nc.vector.tensor_copy(pair[:, q, :, 1].bitcast(F32), gates[:])
                    then(nc.vector.tensor_tensor(counted[:], counted[:], picked[:], ALU.add))
                    nc.vector.tensor_scalar(token[:], token[:], float(P), None, ALU.add).then_inc(s["pair_ready"], 1)
                    dve.wait_ge(s["pair_ready"], n + 1)

                def step(n, q, first, last):
                    if first:
                        moments_of(0, 0)
                        normalise(0, 0)
                        split_weights(sg_lo, sg_hi, 0)
                        x_low(0)
                        moments_of(1, 1)
                        split_weights(su_lo, su_hi, 1)
                        normalise(1, 1)
                        split_weights(sd_lo, sd_hi, 2)
                        dve.wait_ge(s["const_in"], 48)
                        dve.wait_ge(s["bias_in"], 16)
                        nc.vector.memset(counted[:], 0.0)
                        then(nc.vector.tensor_copy(token[:], columns[:, 0:1]))
                        nc.vector.memset(best_f[:], 0.0).then_inc(s["consts_ready"], 1)
                    else:
                        hidden_low(n - 1)
                        if not last:
                            normalise(n + 1, 1 - q)
                    dve.wait_ge(s["squashed"], n + 1)
                    then(nc.vector.scalar_tensor_tensor(act_half[:], act_half[:], 1.0, psum[:, GATE], ALU.add, ALU.mult))
                    if not first:
                        assign(n - 1, 1 - q)
                    dve.wait_ge(s["up_filled"], n + 1)
                    nc.vector.scalar_tensor_tensor(hidden[:], act_half[:], 0.5, psum[:, UP], ALU.mult, ALU.mult).then_inc(s["hidden_ready"], 1)
                    if not last:
                        x_low(n + 1)
                    choose(n)
                    if not first:
                        add(n - 1, 1 - q)
                    if not last:
                        moments_of(n + 2, q)

                step(0, 0, True, False)
                start = count[0]
                with dve.Fori(0, (TILES - 2) // 2) as i:
                    base[0], count[0] = i * ROUTE_STEPS + start, 0
                    step(2 * i + 1, 1, False, False)
                    step(2 * i + 2, 0, False, False)
                    assert count[0] == ROUTE_STEPS, count[0]
                base[0], count[0] = (TILES - 2) // 2 * ROUTE_STEPS + start, 0
                step(TILES - 1, 1, False, True)
                hidden_low(TILES - 1)
                assign(TILES - 1, 1)
                add(TILES - 1, 1)

                dve.wait_ge(s["counts_filled"], 1)
                then(nc.vector.tensor_scalar(before[:, 0], psum[:, RANK, 0:E], float(P - 1), None, ALU.add))
                then(nc.vector.tensor_copy(counts_i[:, 0], before[:, 0]))
                then(nc.vector.tensor_scalar(counts_i[:, 1], counts_i[:, 0], P.bit_length() - 1, None, ALU.logical_shift_right))
                then(nc.vector.tensor_copy(n_tiles[:], counts_i[:, 1]))
                then(nc.vector.tensor_copy(ends[:, 0], n_tiles[:]))
                src = 0
                for shift in (1, 2, 4):
                    then(nc.vector.tensor_copy(ends[:, 1 - src, 0:shift], ends[:, src, 0:shift]))
                    then(nc.vector.tensor_tensor(ends[:, 1 - src, shift:E], ends[:, src, shift:E], ends[:, src, 0:E - shift], ALU.add))
                    src = 1 - src
                then(nc.vector.tensor_scalar(before[:, 0], ends[:, src], columns[:, 0:1], None, ALU.is_le))
                then(nc.vector.tensor_tensor_reduce(before[:, 1, 0:E - 1], before[:, 0, 0:E - 1], n_tiles[:, 0:E - 1], 1.0, 0.0, ALU.mult, ALU.add, table_f[:, 1:2]))
                then(nc.vector.tensor_reduce(table_f[:, 0:1], before[:, 0, 0:E - 1], mybir.AxisListType.X, ALU.add))
                then(nc.vector.tensor_tensor(table_f[:, 2:3], columns[:, 0:1], table_f[:, 1:2], ALU.subtract))
                then(nc.vector.tensor_scalar(table_f[:, 2:3], table_f[:, 2:3], float(P), None, ALU.mult))
                then(nc.vector.scalar_tensor_tensor(table_f[:, 1:2], table_f[:, 0:1], float(TOKENS), table_f[:, 2:3], ALU.mult, ALU.add))
                nc.vector.tensor_copy(table[:], table_f[:, 0:2]).then_inc(s["table_ready"], 1)


def experts_phase(nc, k, xn_rows, out, halves, pairs, tile_table):
    with ExitStack() as ctx:
        def sb(name, shape, dt=F32):
            return ctx.enter_context(nc.sbuf_tensor("e_" + name, shape, dt))

        def sem(name):
            return ctx.enter_context(nc.semaphore("e_" + name))

        CHUNKS = E * DC
        PER_EXPERT = 2 * DC * 16
        w_hi, w_lo = sb("w_hi", [P, CHUNKS, CW], F32R), sb("w_lo", [P, CHUNKS, CW], F32R)
        ident = sb("ident", [P, P])
        table = sb("table", [1, 2 * P], I32)
        pairs_sb = sb("pairs", [P, VISITS, 2], I32)
        take, current = sb("take", [P, 2], I32), sb("current", [P, 2, 2], I32)
        x = sb("x", [P, 2, D])
        xT_hi, xT_lo = sb("xT_hi", [P, D], F32R), sb("xT_lo", [P, D], F32R)
        hidden = sb("hidden", [P, F])
        hT_hi, hT_lo = sb("hT_hi", [P, F], F32R), sb("hT_lo", [P, F], F32R)
        y = sb("y", [P, D])
        psum = ctx.enter_context(nc.psum_tensor("e_psum", [P, 8, 512], F32))
        XT, GATE_UP, HT, DOWN = 0, 1, 3, 4

        names = "const_in table_in w_in cleared pair_in take_ready current_ready x_used xT_filled xT_rounded xT_split gate_filled squashed vec_step "
        names += "hidden_ready hT_filled hT_rounded hT_split down_filled y_ready y_used added passed"
        s = {n: sem(n) for n in names.split()}
        x_in = [sem(f"x_in{i}") for i in range(2)]

        def pipeline(eng, step):
            step(0, 0, True, False)
            with eng.Fori(0, (VISITS - 2) // 2) as i:
                step(2 * i + 1, 1, False, False)
                step(2 * i + 2, 0, False, False)
            step(VISITS - 1, 1, False, True)

        def per_slot(n, q):
            return (n - q) * 8 + 16

        with nc.Block() as block:
            @block.sync
            def _(sp):
                sp.dma_start(ident[:], k["ident"]).then_inc(s["const_in"], 16)
                sp.dma_start(table[:], tile_table.rearrange("(a n) -> a n", a=1)).then_inc(s["table_in"], 16)

                def load_weights(e, c):
                    for i, w in enumerate((w_hi, w_lo)):
                        sp.dma_start(w[:, DC * e + c].bitcast(F32), halves[DC * e + c, i]).then_inc(s["w_in"], 16)

                def load_pairs(start, end):
                    with sp.Fori(start, end) as n:
                        row = sp.value_load(table[0:1, bass.ds(2 * n + 1, 1)], min_val=0, max_val=SLOTS - P)
                        sp.dma_start(pairs_sb[:, bass.ds(n, 1)], pairs[bass.ds(row, P)].unsqueeze(1)).then_inc(s["pair_in"], 16)
                        sp.wait_ge(s["pair_in"], 16 * n + 16)
                        alone(sp, s["passed"])

                load_weights(0, 0)
                load_weights(0, 1)
                sp.wait_ge(s["table_in"], 16)
                load_pairs(0, 2)
                load_weights(0, 2)
                load_weights(0, 3)
                load_pairs(2, VISITS // E)
                sp.wait_ge(s["w_in"], PER_EXPERT)
                for e in range(1, E):
                    tiles = VISITS // E * e
                    for c in range(DC):
                        load_weights(e, c)
                        load_pairs(tiles + 2 * c, tiles + (2 * c + 2 if c + 1 < DC else VISITS // E))
                        sp.wait_ge(s["w_in"], PER_EXPERT * e + 32 * (c + 1))

            @block.gpsimd
            def _(pool):
                pool.wait_ge(s["cleared"], 1)

                def fetch(n, q):
                    pool.wait_ge(s["pair_in"], 16 * n + 16)
                    alone(pool, s["passed"])
                    pool.wait_ge(s["x_used"], n + 1)
                    alone(pool, s["passed"])
                    nc.gpsimd.tensor_copy(take[:, q:q + 1], pairs_sb[:, bass.ds(n, 1), 0]).then_inc(s["take_ready"], 1)
                    pool.wait_ge(s["take_ready"], n + 1)
                    alone(pool, s["passed"])
                    pool.indirect_dma_start(out=x[:, q], out_offset=None, in_=xn_rows, in_offset=bass.IndirectOffsetOnAxis(ap=take[:, q:q + 1], axis=0),
                                            bounds_check=TOKENS - 1, oob_is_err=False).then_inc(x_in[q], 16)

                def give(n, q):
                    pool.wait_ge(s["y_ready"], n + 2)
                    alone(pool, s["passed"])
                    pool.indirect_dma_start(out=out, out_offset=bass.IndirectOffsetOnAxis(ap=current[:, q, 0:1], axis=0), in_=y[:], in_offset=None,
                                            bounds_check=TOKENS - 1, oob_is_err=False, compute_op=ALU.add).then_inc(s["added"], 16)

                def given(n):
                    pool.wait_ge(s["added"], 16 * n + 16)
                    pool.sem_inc(s["y_used"], 1)
                    alone(pool, s["passed"])

                def current_pairs(n, q):
                    nc.gpsimd.tensor_copy(current[:, q], pairs_sb[:, bass.ds(n, 1)].rearrange("p a w -> p (a w)")).then_inc(s["current_ready"], 1)

                def step(n, q, fetches=True, goes_on=True):
                    give(n, q)
                    if fetches:
                        fetch(n + 4, q)
                    given(n)
                    if goes_on:
                        current_pairs(n + 2, q)

                pool.sem_inc(s["y_used"], 1)
                fetch(0, 0)
                fetch(1, 1)
                current_pairs(0, 0)
                current_pairs(1, 1)
                fetch(2, 0)
                fetch(3, 1)
                with pool.Fori(0, (VISITS - 4) // 2) as i:
                    step(2 * i, 0)
                    step(2 * i + 1, 1)
                step(VISITS - 4, 0, fetches=False)
                step(VISITS - 3, 1, fetches=False)
                step(VISITS - 2, 0, fetches=False, goes_on=False)
                step(VISITS - 1, 1, fetches=False, goes_on=False)

            @block.scalar
            def _(act):
                act.sem_inc(s["y_ready"], 1)

                def x_high(n):
                    act.wait_ge(s["xT_filled"], n + 1)
                    nc.scalar.activation(xT_hi[:], psum[:, XT], ACT.Copy).then_inc(s["xT_rounded"], 1)

                def weigh(n, q):
                    act.wait_ge(s["down_filled"], n + 1)
                    act.wait_ge(s["current_ready"], n + 1)
                    act.wait_ge(s["y_used"], n + 1)
                    nc.scalar.activation(y[:], psum[:, DOWN], ACT.Copy, scale=current[:, q, 1:2].bitcast(F32)).then_inc(s["y_ready"], 1)

                def step(n, q, first, last):
                    if first:
                        x_high(0)
                    act.wait_ge(s["gate_filled"], n + 1)
                    nc.scalar.activation(hidden[:], psum[:, GATE_UP, 0:F], ACT.Tanh, scale=0.5).then_inc(s["squashed"], 1)
                    if not last:
                        x_high(n + 1)
                    if not first:
                        weigh(n - 1, 1 - q)
                    act.wait_ge(s["hT_filled"], n + 1)
                    nc.scalar.activation(hT_hi[:], psum[:, HT, 0:F], ACT.Copy).then_inc(s["hT_rounded"], 1)

                pipeline(act, step)
                weigh(VISITS - 1, 1)

            @block.tensor
            def _(pe):
                pe.wait_ge(s["const_in"], 16)
                pe.wait_ge(s["table_in"], 16)

                def x_transposes(n, q):
                    pe.wait_ge(x_in[q], per_slot(n, q))
                    for c in range(DC):
                        last = nc.tensor.transpose(psum[:, XT, P * c:P * (c + 1)], x[:, q, P * c:P * (c + 1)], ident[:])
                    last.then_inc(s["xT_filled"], 1)

                def expert_of(n):
                    return pe.value_load(table[0:1, bass.ds(2 * n, 1)], min_val=0, max_val=E - 1)

                def three(out, lh, ll, rh, rl, start, stop):
                    nc.tensor.matmul(out, lh, rh, start=start, stop=False)
                    nc.tensor.matmul(out, lh, rl, start=False, stop=False)
                    return nc.tensor.matmul(out, ll, rh, start=False, stop=stop)

                def down(n, e):
                    pe.wait_ge(s["hT_rounded"], n + 1)
                    pe.wait_ge(s["hT_split"], n + 1)
                    pe.wait_ge(s["y_ready"], n + 1)
                    for j in range(FC):
                        at = bass.ds(DC * e + FC * j, FC)
                        last = three(psum[:, DOWN], hT_hi[:, P * j:P * (j + 1)], hT_lo[:, P * j:P * (j + 1)],
                                     w_hi[:, at, 2 * F:CW], w_lo[:, at, 2 * F:CW], j == 0, j == FC - 1)
                    last.then_inc(s["down_filled"], 1)

                def gate_up(n, e):
                    pe.wait_ge(s["xT_rounded"], n + 1)
                    pe.wait_ge(s["xT_split"], n + 1)
                    for c in range(DC):
                        at = bass.ds(DC * e + c, 1)
                        mm = three(psum[:, GATE_UP], xT_hi[:, P * c:P * (c + 1)], xT_lo[:, P * c:P * (c + 1)],
                                   w_hi[:, at, 0:2 * F], w_lo[:, at, 0:2 * F], c == 0, c == DC - 1)
                    mm.then_inc(s["gate_filled"], 1)

                def weights_there(e):
                    pe.wait_ge(s["w_in"], PER_EXPERT * e + PER_EXPERT)

                def step(n, q, first, last):
                    if first:
                        x_transposes(0, 0)
                        e = expert_of(0)
                        weights_there(e)
                        gate_up(0, e)
                    if not last:
                        x_transposes(n + 1, 1 - q)
                        e = expert_of(n + 1)
                        weights_there(e)
                    if not first:
                        down(n - 1, expert_of(n - 1))
                    pe.wait_ge(s["hidden_ready"], n + 1)
                    for j in range(FC):
                        mm = nc.tensor.transpose(psum[:, HT, P * j:P * (j + 1)], hidden[:, j:F:FC], ident[:])
                    mm.then_inc(s["hT_filled"], 1)
                    if not last:
                        gate_up(n + 1, e)

                pipeline(pe, step)
                down(VISITS - 1, expert_of(VISITS - 1))

            @block.vector
            def _(dve):
                nc.vector.memset(x[:], 0.0).then_inc(s["cleared"], 1)
                dve.sem_inc(s["x_used"], 2)

                def x_low(n):
                    dve.wait_ge(s["xT_rounded"], n + 1)
                    dve.sem_inc(s["x_used"], 1)
                    nc.vector.tensor_tensor(xT_lo[:], psum[:, XT], xT_hi[:].bitcast(F32), ALU.subtract).then_inc(s["xT_split"], 1)

                def step(n, q, first, last):
                    if first:
                        x_low(0)
                    dve.wait_ge(s["squashed"], n + 1)
                    nc.vector.scalar_tensor_tensor(hidden[:], hidden[:], 1.0, psum[:, GATE_UP, 0:F], ALU.add, ALU.mult).then_inc(s["vec_step"], 1)
                    dve.wait_ge(s["vec_step"], n + 1)
                    nc.vector.scalar_tensor_tensor(hidden[:], hidden[:], 0.5, psum[:, GATE_UP, F:2 * F], ALU.mult, ALU.mult).then_inc(s["hidden_ready"], 1)
                    if not last:
                        x_low(n + 1)
                    dve.wait_ge(s["hT_rounded"], n + 1)
                    nc.vector.tensor_tensor(hT_lo[:], psum[:, HT, 0:F], hT_hi[:].bitcast(F32), ALU.subtract).then_inc(s["hT_split"], 1)

                pipeline(dve, step)


ROUTE_STEPS = 28


def build(nc, x, ctx, mask, wq, wk, wv, wo, wr, wg, wu, wd, sg, su, sd, expert_bias, out):
    def scratch(name, shape, dt=F32):
        return nc.dram_tensor(name, shape, dt, kind="Internal").ap()

    def tiles(rows):
        return rows.rearrange("(t p) d -> t p d", p=P)

    x2, xn = scratch("x2_rows", (TOKENS, D)), scratch("xn_rows", (TOKENS, D))
    halves = scratch("w_halves", (E * DC, 2, P, CW))
    pairs, tile_table = scratch("pairs", (SLOTS, 2), I32), scratch("tile_table", (2 * P,), I32)
    out_rows = out.rearrange("b l d -> (b l) d")
    k = tables(nc)
    attention_phase(nc, k, tiles(x.rearrange("b l d -> (b l) d")), tiles(ctx.rearrange("b l d -> (b l) d")), mask, wq, wk, wv, wo, tiles(x2))
    shared_phase(nc, k, tiles(x2), tiles(xn), tiles(out_rows), wr, sg, su, sd, expert_bias, wg, wu, wd, pairs, halves, tile_table)
    experts_phase(nc, k, xn, out_rows, halves, pairs, tile_table)


_INS = ["x", "ctx_1024", "mask_1x1xSxS2_ik0"] + [f"L0_xattn_{n}" for n in ("wq", "wk", "wv", "wo")]
_INS += [f"L0_ffn_{n}" for n in ("Wr", "Wg", "Wu", "Wd", "Sg", "Su", "Sd", "expert_bias")]


def kernel(**inputs):
    import numpy as _np
    import concourse.bacc as _bacc
    from concourse import mybir as _mybir
    from concourse.bass_utils import run_bass_kernel_spmd as _run

    nc = _bacc.Bacc("TRN2", target_bir_lowering=False, num_devices=1)
    arrays, args = {}, []
    for name in _INS:
        a = _np.ascontiguousarray(inputs[name])
        arrays[f"in_{name}"] = a
        args.append(nc.dram_tensor(f"in_{name}", a.shape, _mybir.dt.from_np(a.dtype), kind="ExternalInput").ap())
    out = nc.dram_tensor("out_0", (B, L, D), _mybir.dt.float32, kind="ExternalOutput").ap()
    build(nc, *args, out)
    return _run(nc, [arrays], core_ids=[0]).results[0]["out_0"]
```
